# Optimizing a Trainium2 kernel written in Bass

```python
import numpy as np
import jax
import jax.numpy as jnp

def _softmax(x, axis=-1):
    return jax.nn.softmax(x, axis=axis)

def _gelu(x):
    return jax.nn.gelu(x, approximate=True)

def _silu(x):
    return jax.nn.silu(x)

def _sigmoid(x):
    return jax.nn.sigmoid(x)

def _layernorm(x, axis=-1, eps=1e-05):
    m = jnp.mean(x, axis=axis, keepdims=True)
    v = jnp.var(x, axis=axis, keepdims=True)
    return (x - m) / jnp.sqrt(v + eps)

def _scatter_add(tgt, idx, src, axis=0):
    return tgt.at[idx].add(src)

def _segment_sum(src, seg, n):
    return jax.ops.segment_sum(src, seg, n)
kernel_name = 'mk_adj_ffn_d1_adj_r2_cdc6bc'

def setup_inputs(seed: int=0):
    np.random.seed(seed)
    _w = jnp.asarray

    def _rec_inputs():
        import jax
        import jax.numpy as jnp
        _gk = jax.random.key(seed)
        x = -0.0005207 + 1.001 * jax.random.normal(jax.random.fold_in(_gk, 1), (8, 1024, 128), jnp.float32)
        _a = jax.random.bernoulli(jax.random.fold_in(_gk, 2), 0.00390625, (1024, 1024))
        _a = jnp.logical_or(_a, jnp.swapaxes(_a, -1, -2))
        _a = jnp.logical_or(_a, jnp.eye(1024, dtype=bool))
        adj = _a.astype(jnp.int32)
        return (x, adj)
    x, adj = _rec_inputs()

    def _L0_gnn_setup():
        import jax, jax.numpy as jnp
        import numpy as np
        import math
        CHUNK = 128
        NUM_HEADS = 4
        EPS = 1e-05
        key = jax.random.key(seed)
        ks = jax.random.split(key, 12)
        B, N, F = (4, 1024, 128)
        x = jax.random.normal(ks[0], (B, N, F), dtype=jnp.float32)
        adj_matrix = jax.random.randint(ks[1], (N, N), 0, 2, dtype=jnp.int32)
        s = 1.0 / math.sqrt(F)
        Wq = jax.random.normal(ks[2], (F, F), dtype=jnp.float32) * s
        bq = jnp.zeros((F,), dtype=jnp.float32)
        Wk = jax.random.normal(ks[3], (F, F), dtype=jnp.float32) * s
        bk = jnp.zeros((F,), dtype=jnp.float32)
        Wv = jax.random.normal(ks[4], (F, F), dtype=jnp.float32) * s
        bv = jnp.zeros((F,), dtype=jnp.float32)
        Wo = jax.random.normal(ks[5], (F, F), dtype=jnp.float32) * s
        bo = jnp.zeros((F,), dtype=jnp.float32)
        gamma = jnp.ones((F,), dtype=jnp.float32)
        beta = jnp.zeros((F,), dtype=jnp.float32)
        return {'x': x, 'adj_matrix': adj_matrix, 'Wq': Wq, 'bq': bq, 'Wk': Wk, 'bk': bk, 'Wv': Wv, 'bv': bv, 'Wo': Wo, 'bo': bo, 'gamma': gamma, 'beta': beta}
    _L0_gnn_all = _L0_gnn_setup()
    _L0_gnn_in = {k: v for k, v in _L0_gnn_all.items() if k in ('Wq', 'bq', 'Wk', 'bk', 'Wv', 'bv', 'Wo', 'bo', 'gamma', 'beta')}
    del _L0_gnn_all

    def _L0_ffn_setup():
        import jax, jax.numpy as jnp
        import numpy as np
        B, T, D, H, E = (16, 2048, 128, 256, 8)
        key = jax.random.key(seed)
        ks = jax.random.split(key, 5)
        x = jax.random.normal(ks[0], (B, T, D), dtype=jnp.float32)
        gate_w = jax.random.normal(ks[1], (D, E), dtype=jnp.float32) * 0.02
        gate_b = jnp.zeros((E,), dtype=jnp.float32)
        W1 = jax.random.normal(ks[2], (E, D, H), dtype=jnp.float32) * 0.02
        b1 = jnp.zeros((E, H), dtype=jnp.float32)
        W2 = jax.random.normal(ks[3], (E, H, D), dtype=jnp.float32) * 0.02
        b2 = jnp.zeros((E, D), dtype=jnp.float32)
        return {'x': x, 'gate_w': gate_w, 'gate_b': gate_b, 'W1': W1, 'b1': b1, 'W2': W2, 'b2': b2}
    _L0_ffn_all = _L0_ffn_setup()
    _L0_ffn_in = {k: v for k, v in _L0_ffn_all.items() if k in ('gate_w', 'gate_b', 'W1', 'b1', 'W2', 'b2')}
    del _L0_ffn_all
    return {'x': x, 'adj': adj, 'L0_gnn_Wq': _L0_gnn_in['Wq'], 'L0_gnn_bq': _L0_gnn_in['bq'], 'L0_gnn_Wk': _L0_gnn_in['Wk'], 'L0_gnn_bk': _L0_gnn_in['bk'], 'L0_gnn_Wv': _L0_gnn_in['Wv'], 'L0_gnn_bv': _L0_gnn_in['bv'], 'L0_gnn_Wo': _L0_gnn_in['Wo'], 'L0_gnn_bo': _L0_gnn_in['bo'], 'L0_gnn_gamma': _L0_gnn_in['gamma'], 'L0_gnn_beta': _L0_gnn_in['beta'], 'L0_ffn_gate_w': _L0_ffn_in['gate_w'], 'L0_ffn_gate_b': _L0_ffn_in['gate_b'], 'L0_ffn_W1': _L0_ffn_in['W1'], 'L0_ffn_b1': _L0_ffn_in['b1'], 'L0_ffn_W2': _L0_ffn_in['W2'], 'L0_ffn_b2': _L0_ffn_in['b2']}

def reference(x, adj, L0_gnn_Wq, L0_gnn_bq, L0_gnn_Wk, L0_gnn_bk, L0_gnn_Wv, L0_gnn_bv, L0_gnn_Wo, L0_gnn_bo, L0_gnn_gamma, L0_gnn_beta, L0_ffn_gate_w, L0_ffn_gate_b, L0_ffn_W1, L0_ffn_b1, L0_ffn_W2, L0_ffn_b2):
    import jax
    import jax.numpy as jnp

    def _L0_gnn_ref(x, adj_matrix, Wq, bq, Wk, bk, Wv, bv, Wo, bo, gamma, beta):
        import jax, jax.numpy as jnp
        import numpy as np
        import math
        CHUNK = 128
        NUM_HEADS = 4
        EPS = 1e-05
        B, N, Fin = x.shape
        H = NUM_HEADS
        Dout = Wq.shape[0]
        Dh = Dout // H
        Nc = N // CHUNK
        q = (x @ Wq.T + bq).reshape(B, N, H, Dh).transpose(0, 2, 1, 3)
        k = (x @ Wk.T + bk).reshape(B, N, H, Dh).transpose(0, 2, 1, 3)
        v = (x @ Wv.T + bv).reshape(B, N, H, Dh).transpose(0, 2, 1, 3)
        kc = k.reshape(B, H, Nc, CHUNK, Dh)
        vc = v.reshape(B, H, Nc, CHUNK, Dh)
        scores = jnp.einsum('bhnd,bhjcd->bhnjc', q, kc) / jnp.sqrt(jnp.asarray(Dh, dtype=q.dtype))
        scores = jnp.clip(scores, -10.0, 10.0)
        mask = adj_matrix.reshape(N, Nc, CHUNK)[None, None]
        scores = jnp.where(mask == 0, jnp.asarray(-10.0, scores.dtype), scores)
        attn = jax.nn.softmax(scores, axis=-1)
        ctx = jnp.einsum('bhnjc,bhjcd->bhnd', attn, vc)
        ctx = ctx.transpose(0, 2, 1, 3).reshape(B, N, Dout)
        out = ctx @ Wo.T + bo
        out = out + x
        mu = jnp.mean(out, axis=-1, keepdims=True)
        var = jnp.mean(jnp.square(out - mu), axis=-1, keepdims=True)
        out = (out - mu) * jax.lax.rsqrt(var + EPS) * gamma + beta
        return out

    def _L0_ffn_ref(x, gate_w, gate_b, W1, b1, W2, b2):
        import jax, jax.numpy as jnp
        import numpy as np
        B, T, D, H, E = (16, 2048, 128, 256, 8)
        Bb, Tt, Dd = x.shape
        Ee = gate_w.shape[1]
        xf = x.reshape(-1, Dd)
        N = xf.shape[0]
        logits = xf @ gate_w + gate_b
        probs = jax.nn.softmax(logits, axis=-1)
        top2_vals, top2_idx = jax.lax.top_k(probs, 2)
        cw = jnp.zeros((N, Ee), dtype=xf.dtype).at[jnp.arange(N)[:, None], top2_idx].add(top2_vals)

        def step(acc, params):
            w1, bb1, w2, bb2, we = params
            h = jax.nn.gelu(xf @ w1 + bb1, approximate=False)
            y = h @ w2 + bb2
            return (acc + we[:, None] * y, None)
        out, _ = jax.lax.scan(step, jnp.zeros_like(xf), (W1, b1, W2, b2, cw.T))
        return out.reshape(Bb, Tt, Dd)
    x = x + _L0_gnn_ref(_layernorm(x, axis=-1), adj, L0_gnn_Wq, L0_gnn_bq, L0_gnn_Wk, L0_gnn_bk, L0_gnn_Wv, L0_gnn_bv, L0_gnn_Wo, L0_gnn_bo, L0_gnn_gamma, L0_gnn_beta)
    x = x + _L0_ffn_ref(_layernorm(x, axis=-1), L0_ffn_gate_w, L0_ffn_gate_b, L0_ffn_W1, L0_ffn_b1, L0_ffn_W2, L0_ffn_b2)
    return x

_drawn_inputs = setup_inputs


def setup_inputs(seed=0):
    import zlib

    import numpy as np

    out = dict(_drawn_inputs(seed))
    spreads = {'L0_gnn_bq': (0.0, 0.573),
     'L0_gnn_bk': (0.0, 0.8),
     'L0_gnn_bv': (0.0, 0.1),
     'L0_gnn_bo': (0.0, 0.332),
     'L0_gnn_gamma': (1.0, 0.2),
     'L0_gnn_beta': (0.0, 0.1),
     'L0_ffn_gate_b': (0.0, 0.798),
     'L0_ffn_b1': (0.0, 0.8),
     'L0_ffn_b2': (0.0, 0.603)}
    factors = {'L0_ffn_gate_w': 4.645, 'L0_ffn_W1': 8.0, 'L0_ffn_W2': 8.0}
    for name, (base, spread) in spreads.items():
        noise = np.random.default_rng([zlib.crc32(name.encode()), seed]).standard_normal(out[name].shape)
        drawn = base * np.exp(spread * noise) if base else spread * noise
        out[name] = jnp.asarray(drawn.astype(out[name].dtype))
    for name, factor in factors.items():
        out[name] = (out[name] * factor).astype(out[name].dtype)
    return out
```

```python
from contextlib import ExitStack

import concourse.bass as bass
from concourse import mybir

ALU = mybir.AluOpType
ACT = mybir.ActivationFunctionType
AX = mybir.AxisListType
F32 = mybir.dt.float32
F16 = mybir.dt.float16
BF16 = mybir.dt.bfloat16
I32 = mybir.dt.int32
U32 = mybir.dt.uint32

P = 128
WSCALE = 256.0
EPS = 1e-5
LIMIT = 10.0
RSQRT_MAGIC = float(0x5F3759DF - 0x400000)
NEWTON = 3
NEWTON_OPS = 4 * NEWTON
STAT_STEPS = 6


def gnn_moe(nc, x, adj, Wq, bq, Wk, bk, Wv, bv, Wo, bo, gamma, beta, gate_w, gate_b, W1, b1, W2, b2, out):
    NB, N, D = x.shape
    T = N // P
    HEADS, DH = 4, 32
    E, _, HID = W1.shape
    KH = HID // P
    HALF = N // 2
    TH = T // 2
    STEPS = 2 * T
    STACKS = 8 * HEADS
    assert D == P and HEADS * DH == D and N == 1024 and HALF == 512 and KH == 2 and E == 8
    QSCALE = float(DH) ** -0.5

    ctx = ExitStack()
    with ctx:
        def sb(name, shape, dt):
            return ctx.enter_context(nc.sbuf_tensor(name, shape, dt))

        def sem(name):
            return ctx.enter_context(nc.semaphore(name))

        ident = sb("ident", [P, P], F32)
        identb = sb("identb", [P, P], BF16)
        three_halves = sb("three_halves", [P, T], F32)
        expert_no = sb("expert_no", [P, E], F32)
        vec_raw = sb("vec_raw", [E * KH + 3, P], F32)
        vec = sb("vec", [P, E * KH + 3], F32)
        bq_scaled = sb("bq_scaled", [P, 1], F32)
        bv_total = sb("bv_total", [P, 1], F32)
        wqkv_hi = sb("wqkv_hi", [P, 3, P], F16)
        wqkv_lo = sb("wqkv_lo", [P, 3, P], F16)
        woT = sb("woT", [P, P], F32)
        rows_bc = sb("rows_bc", [P, 3, P], F32)
        gate_b_bc = sb("gate_b_bc", [P, E], F32)
        gate_raw = sb("gate_raw", [P, E], F32)
        gate_hi = sb("gate_hi", [P, E], F16)
        gate_lo = sb("gate_lo", [P, E], F16)
        w1_hi = sb("w1_hi", [P, E, HID], F16)
        w1_lo = sb("w1_lo", [P, E, HID], F16)
        w2_hi = sb("w2_hi", [P, E, KH, P], F16)
        w2_lo = sb("w2_lo", [P, E, KH, P], F16)
        b2_sb = sb("b2_sb", [E, P], F32)
        limit = sb("limit", [P, T, N], BF16)
        x1 = sb("x1", [P, NB, T * P], F32)
        adj_raw = x1[:, :, :].bitcast(I32)
        w_raw = [x1[:, NB - 4 + 2 * i:NB - 2 + 2 * i, :].rearrange("p b n -> p (b n)") for i in range(2)]
        xin = sb("xin", [P, T, P], F32)
        xn = sb("xn", [P, T, P], F32)
        xn_bo = sb("xn_bo", [P, 2, T, P], F32)
        x_beta = sb("x_beta", [P, 2, T, P], F32)
        xT_hi = sb("xT_hi", [P, 2, HALF], F16)
        xT_lo = sb("xT_lo", [P, 2, HALF], F16)
        qk = sb("qk", [P, 4, HALF], F32)
        qk_hi = sb("qk_hi", [P, 4, HALF], F16)
        qk_lo = sb("qk_lo", [P, 4, HALF], F16)
        qstack = sb("qstack", [P, 2, HEADS, N], F16)
        kstack = sb("kstack", [P, 2, HEADS, N], F16)
        v_sb = sb("v_sb", [P, 2, T, HEADS, DH + 1], F32)
        clip_buf = sb("clip_buf", [P, 2 * HEADS * HALF], F32)
        prob_buf = sb("prob_buf", [P, 2 * HEADS * HALF], F32)
        clipped = clip_buf[:, :].rearrange("p (r h n) -> p r h n", r=2, h=HEADS)
        probs = prob_buf[:, :].rearrange("p (r h n) -> p r h n", r=2, h=HEADS)
        mask20 = clip_buf[:, :].bitcast(BF16).rearrange("p (t k q) -> p t k q", t=T, k=T)
        pv_sb = sb("pv_sb", [P, 2, TH, HEADS, DH + 1], F32)
        rden = sb("rden", [P, 2, TH * HEADS], F32)
        scaled = sb("scaled", [P, TH * HEADS, DH], F32)
        ctxn = sb("ctxn", [P, 2, TH, P], F32)
        ctxT = sb("ctxT", [P, HALF], F32)
        res = sb("res", [P, TH, P], F32)
        y_sb = sb("y_sb", [P, TH, P], F32)
        wqkvo_raw = y_sb
        stats = sb("stats", [P, T, 6], F32)
        mean = sb("mean", [P, T], F32)
        msq = sb("msq", [P, T], F32)
        var_e = sb("var_e", [P, T], F32)
        rstd = sb("rstd", [P, T], F32)
        newt = sb("newt", [P, T], F32)
        stats2 = sb("stats2", [P, TH, 6], F32)
        mean2 = sb("mean2", [P, TH], F32)
        msq2 = sb("msq2", [P, TH], F32)
        var_e2 = sb("var_e2", [P, TH], F32)
        rstd2 = sb("rstd2", [P, TH], F32)
        newt2 = sb("newt2", [P, TH], F32)
        hid = clip_buf[:, 0:2 * KH * HALF].rearrange("p (r k n) -> p r k n", r=2, k=KH)
        acc = clip_buf[:, 2 * KH * HALF:2 * KH * HALF + 2 * HALF].rearrange("p (r t d) -> p r t d", r=2, t=TH)
        hid_hi = prob_buf[:, 0:2 * KH * HALF].bitcast(F16).rearrange("p (r k n) -> p r k n", r=4, k=KH)
        hid_lo = prob_buf[:, 2 * KH * HALF:4 * KH * HALF].bitcast(F16).rearrange("p (r k n) -> p r k n", r=4, k=KH)
        xn2 = ctxn[:, 0, :, :]
        x2T_hi = qk[:, 0:2, :].rearrange("p a n -> p (a n)").bitcast(F16)[:, 0:2 * HALF].rearrange("p (r n) -> p r n", r=2)
        x2T_lo = qk[:, 2:4, :].rearrange("p a n -> p (a n)").bitcast(F16)[:, 0:2 * HALF].rearrange("p (r n) -> p r n", r=2)
        logit = sb("logit", [P, TH, E], F32)
        top = sb("top", [P, TH, 8], F32)
        top_at = sb("top_at", [P, TH, 8], U32)
        top_no = sb("top_no", [P, TH, 2], F32)
        gsum = sb("gsum", [P, TH], F32)
        gprob = sb("gprob", [P, TH, E], F32)
        gprob_s = sb("gprob_s", [P, TH, E], F32)
        pick = sb("pick", [P, 2, TH, E], F32)
        cw = sb("cw", [P, TH, E], F32)
        cw_s = sb("cw_s", [P, 2, TH, E], F32)
        cwT = scaled[0:E, :, :].rearrange("p g d -> p (g d)")

        score_ps = ctx.enter_context(nc.psum_tensor("score_ps", [P, 4, HALF], F32))
        sum_ps = ctx.enter_context(nc.psum_tensor("sum_ps", [P, 2, HALF], F32))
        side_ps = ctx.enter_context(nc.psum_tensor("side_ps", [P, 2, HALF], F32))

        def side(i):
            return side_ps[:, i, :]

        def side_tiles(i):
            return side_ps[:, i, :].rearrange("p (t d) -> p t d", t=TH)

        consts_ready = sem("consts_ready")
        w_loaded = sem("w_loaded")
        rows_loaded = sem("rows_loaded")
        adj_loaded = [sem(f"adj_loaded{t}") for t in range(T)]
        ffn_w_loaded = sem("ffn_w_loaded")
        w_turned = sem("w_turned")
        w_split = sem("w_split")
        w_low = sem("w_low")
        mask_made = sem("mask_made")
        mask_turned = sem("mask_turned")
        limit_ready = sem("limit_ready")
        ffn_step = sem("ffn_step")
        gate_step = sem("gate_step")
        x_loaded = sem("x_loaded")
        norm_step = sem("norm_step")
        guess_ready = sem("guess_ready")
        newton_step = sem("newton_step")
        rstd_ready = sem("rstd_ready")
        xn_ready = sem("xn_ready")
        xT_done = sem("xT_done")
        xT_hi_ready = sem("xT_hi_ready")
        xT_lo_ready = sem("xT_lo_ready")
        qk_proj_done = sem("qk_proj_done")
        qk_ready = sem("qk_ready")
        qk_hi_ready = sem("qk_hi_ready")
        qk_lo_ready = sem("qk_lo_ready")
        stacked = sem("stacked")
        v_proj_done = sem("v_proj_done")
        v_ready = sem("v_ready")
        x_beta_ready = sem("x_beta_ready")
        xn_bo_ready = sem("xn_bo_ready")
        qk_done = sem("qk_done")
        clip_done = sem("clip_done")
        exp_done = sem("exp_done")
        pv_done = sem("pv_done")
        pv_copied = sem("pv_copied")
        rden_ready = sem("rden_ready")
        scaled_ready = sem("scaled_ready")
        ctx_added = sem("ctx_added")
        ctxn_turned = sem("ctxn_turned")
        ctxT_ready = sem("ctxT_ready")
        wo_done = sem("wo_done")
        res_ready = sem("res_ready")
        norm2_step = sem("norm2_step")
        guess2_ready = sem("guess2_ready")
        newton2_step = sem("newton2_step")
        rstd2_ready = sem("rstd2_ready")
        y_ready = sem("y_ready")
        y_scaled = sem("y_scaled")
        x1_ready = sem("x1_ready")
        b_norm_step = sem("b_norm_step")
        b_guess_ready = sem("b_guess_ready")
        b_newton_step = sem("b_newton_step")
        b_rstd_ready = sem("b_rstd_ready")
        xn2_ready = sem("xn2_ready")
        x2T_done = sem("x2T_done")
        x2T_hi_ready = sem("x2T_hi_ready")
        x2T_lo_ready = sem("x2T_lo_ready")
        gate_done = sem("gate_done")
        gate_dve = sem("gate_dve")
        gate_exp = sem("gate_exp")
        cw_ready = sem("cw_ready")
        cwT_done = sem("cwT_done")
        cwT_ready = sem("cwT_ready")
        b2_done = sem("b2_done")
        acc_start = sem("acc_start")
        z_done = sem("z_done")
        gelu_done = sem("gelu_done")
        hid_hi_ready = sem("hid_hi_ready")
        hid_lo_ready = sem("hid_lo_ready")
        y_done = sem("y_done")
        acc_done = sem("acc_done")
        stored = [sem(f"stored{i}") for i in range(2)]
        GATE_OPS = 11
        LAST = NB - 1
        CHUNKS = 2 * NB

        def wait(eng, s, value):
            if not isinstance(value, int) or value > 0:
                eng.wait_ge(s, value)

        def bodies(eng, body):
            body(0)
            with eng.Fori(0, (NB - 2) // 2) as i:
                body(2 * i + 1, 1)
                body(2 * i + 2, 0)
            body(LAST)

        x_v = x.rearrange("b (t p) d -> b p t d", t=T)
        out_v = out.rearrange("b (c t p) d -> b c p t d", c=2, t=TH)

        block = ctx.enter_context(nc.Block())

        @block.sync
        def _(sp):
            sp.dma_start(xin[:], x_v[0]).then_inc(x_loaded, 16)
            for i, w in enumerate((Wq, Wk, Wv, Wo)):
                sp.dma_start(wqkvo_raw[:, i, :], w).then_inc(w_loaded, 16)
            sp.dma_start(vec_raw[0:E * KH, :], b1.rearrange("e (k p) -> (e k) p", p=P)).then_inc(w_loaded, 16)
            for i, v in enumerate((bq, bk, bv)):
                sp.dma_start(vec_raw[E * KH + i:E * KH + i + 1, :], v.rearrange("(o d) -> o d", o=1)).then_inc(w_loaded, 16)
            adj_v = adj.rearrange("(t p) k -> p t k", t=T)
            for t in range(T):
                sp.dma_start(adj_raw[:, t, :], adj_v[:, t, :]).then_inc(adj_loaded[t], 16)
            for i, v in enumerate((bo, gamma, beta)):
                sp.dma_start(rows_bc[:, i, :], v.partition_broadcast(P)).then_inc(rows_loaded, 16)
            sp.dma_start(gate_b_bc[:], gate_b.partition_broadcast(P)).then_inc(rows_loaded, 16)
            sp.dma_start(gate_raw[:], gate_w).then_inc(rows_loaded, 16)
            sp.dma_start(b2_sb[:], b2).then_inc(rows_loaded, 16)
            sp.wait_ge(mask_made, T)
            sp.dma_start(w_raw[0].rearrange("p (e h) -> p e h", e=E),
                         W1.rearrange("e d h -> d e h")).then_inc(ffn_w_loaded, 16)
            sp.dma_start(w_raw[1].rearrange("p (e k d) -> p e k d", e=E, k=KH),
                         W2.rearrange("e (k p) d -> p e k d", p=P)).then_inc(ffn_w_loaded, 16)

            def stack(bb, par):
                wait(sp, qk_done, 2 * STEPS * (bb - 1))
                for first, dst, order in ((0, qstack, (0, 0, 1, 1)), (2, kstack, (0, 1, 0, 1))):
                    sp.wait_ge(qk_hi_ready, 4 * bb + first + 2)
                    sp.wait_ge(qk_lo_ready, 4 * bb + first + 2)
                    for r, part in enumerate(order):
                        src = (qk_hi, qk_lo)[part]
                        for h in range(HEADS):
                            sp.dma_start(dst[DH * r:DH * r + DH, par, h, :].rearrange("d (c n) -> d c n", c=2),
                                         src[DH * h:DH * h + DH, first:first + 2, :]).then_inc(stacked, 16)

            stack(0, 0)

            def body(b, par=None):
                par = b % 2 if par is None else par
                if isinstance(b, int) and b == LAST:
                    return
                sp.wait_ge(xn_ready, b + 1)
                sp.wait_ge(x_beta_ready, b + 1)
                sp.dma_start(xin[:], x_v[b + 1]).then_inc(x_loaded, 16)
                stack(b + 1, 1 - par)

            bodies(sp, body)

            def store(b, half):
                sp.wait_ge(acc_done, E * (2 * b + half + 1))
                sp.dma_start(out_v[b, half], acc[:, half, :, :]).then_inc(stored[half], 16)

            with sp.Fori(0, NB) as b:
                store(b, 0)
                store(b, 1)
            sp.wait_ge(stored[0], 16 * NB)
            sp.wait_ge(stored[1], 16 * NB)

        @block.gpsimd
        def _(pool):
            pool.memset(ident[:], 0.0).then_inc(consts_ready, 1)
            pool.memset(identb[:], 0.0).then_inc(consts_ready, 1)
            pool.memset(v_sb[:, :, :, :, DH:DH + 1], 1.0).then_inc(consts_ready, 1)
            pool.memset(three_halves[:], 1.5).then_inc(consts_ready, 1)
            for e in range(E):
                pool.memset(expert_no[:, e:e + 1], float(e)).then_inc(consts_ready, 1)
            pool.wait_ge(consts_ready, 2)
            for m in (ident, identb):
                pool.affine_select(out=m[:], in_=m[:], compare_op=ALU.not_equal, fill=1.0, base=0,
                                   pattern=[[-1, P]], channel_multiplier=1).then_inc(consts_ready, 1)

            def newton(v, y, t, n, step, at, done):
                for i in range(NEWTON):
                    ops = [lambda: pool.tensor_tensor(t[:, 0:n], y[:, 0:n], y[:, 0:n], ALU.mult),
                           lambda: pool.tensor_tensor(t[:, 0:n], t[:, 0:n], v[:, 0:n], ALU.mult),
                           lambda: pool.tensor_tensor(t[:, 0:n], three_halves[:, 0:n], t[:, 0:n], ALU.subtract),
                           lambda: pool.tensor_tensor(y[:, 0:n], y[:, 0:n], t[:, 0:n], ALU.mult)]
                    for k, op in enumerate(ops):
                        j = 4 * i + k
                        if j:
                            pool.wait_ge(step, (NEWTON_OPS - 1) * at + j)
                        if j == NEWTON_OPS - 1:
                            op().then_inc(done, 1)
                        else:
                            op().then_inc(step, 1)

            def prep_rstd(bb):
                pool.wait_ge(guess_ready, bb + 1)
                newton(var_e, rstd, newt, T, newton_step, bb, rstd_ready)

            def prep_low(bb, i):
                pool.wait_ge(qk_hi_ready, 4 * bb + i + 1)
                pool.tensor_tensor(qk_lo[:, i, :], qk[:, i, :], qk_hi[:, i, :], ALU.subtract).then_inc(qk_lo_ready, 1)

            def prep_residuals(bb, par):
                pool.wait_ge(x_loaded, 16 * (bb + 1))
                wait(pool, x1_ready, 2 * (bb - 1))
                pool.tensor_tensor(x_beta[:, par, :, :], xin[:], rows_bc[:, 2:3, :].to_broadcast([P, T, P]),
                                   ALU.add).then_inc(x_beta_ready, 1)
                pool.wait_ge(xn_ready, bb + 1)
                pool.tensor_tensor(xn_bo[:, par, :, :], xn[:], rows_bc[:, 0:1, :].to_broadcast([P, T, P]),
                                   ALU.add).then_inc(xn_bo_ready, 1)

            def normalise(b, s):
                g, k, half = STEPS * b + s, s % T, s // T
                n = 2 * b + half
                pool.wait_ge(rden_ready, g + 1)
                pv = pv_sb[:, s % 2, :, :, 0:DH].rearrange("p t h d -> p (t h) d")
                by = rden[:, s % 2, :].rearrange("p (g o) -> p g o", o=1).to_broadcast([P, TH * HEADS, DH])
                sums = ctxn[:, half, :, :].rearrange("p t (h d) -> p (t h) d", d=DH)
                if k == 0:
                    wait(pool, ctxn_turned, n - 1)
                    pool.tensor_tensor(sums, pv, by, ALU.mult).then_inc(ctx_added, 1)
                else:
                    wait(pool, ctx_added, g)
                    pool.tensor_tensor(scaled[:], pv, by, ALU.mult).then_inc(scaled_ready, 1)
                    pool.wait_ge(scaled_ready, (T - 1) * n + k)
                    pool.tensor_tensor(sums, sums, scaled[:], ALU.add).then_inc(ctx_added, 1)

            def post_rstd(n):
                pool.wait_ge(guess2_ready, n + 1)
                newton(var_e2, rstd2, newt2, TH, newton2_step, n, rstd2_ready)

            def post_final(b, par, half):
                n = 2 * b + half
                pool.wait_ge(y_ready, n + 1)
                pool.tensor_tensor(y_sb[:], y_sb[:], rows_bc[:, 1:2, :].to_broadcast([P, TH, P]),
                                   ALU.mult).then_inc(y_scaled, 1)
                pool.wait_ge(y_scaled, n + 1)
                pool.tensor_tensor(x1[:, b, half * HALF:half * HALF + HALF].rearrange("p (t d) -> p t d", t=TH),
                                   y_sb[:], x_beta[:, par, half * TH:half * TH + TH, :], ALU.add).then_inc(x1_ready, 1)

            pool.wait_ge(rows_loaded, 16 * 6)
            prep_rstd(0)
            for i in range(4):
                prep_low(0, i)
            prep_residuals(0, 0)
            pool.tensor_scalar(gate_raw[:], gate_raw[:], WSCALE, 1.0, ALU.mult, ALU.mult).then_inc(gate_step, 1)
            pool.wait_ge(gate_step, 1)
            pool.tensor_scalar(gate_hi[:], gate_raw[:], 1.0, 1.0, ALU.mult, ALU.mult).then_inc(gate_step, 1)
            pool.wait_ge(gate_step, 2)
            pool.tensor_tensor(gate_lo[:], gate_raw[:], gate_hi[:], ALU.subtract).then_inc(gate_step, 1)

            def split_ffn(n, hi, lo):
                pool.wait_ge(ffn_w_loaded, 16 * 2)
                pool.tensor_scalar(w_raw[n], w_raw[n], WSCALE, 1.0, ALU.mult, ALU.mult).then_inc(ffn_step, 1)
                pool.wait_ge(ffn_step, 3 * n + 1)
                pool.tensor_scalar(hi, w_raw[n], 1.0, 1.0, ALU.mult, ALU.mult).then_inc(ffn_step, 1)
                pool.wait_ge(ffn_step, 3 * n + 2)
                pool.tensor_tensor(lo, w_raw[n], hi, ALU.subtract).then_inc(ffn_step, 1)

            def body(b, par=None):
                par = b % 2 if par is None else par
                first, last = isinstance(b, int) and b == 0, isinstance(b, int) and b == LAST
                for s in range(STEPS):
                    if s >= 2:
                        normalise(b, s - 2)
                    elif not first:
                        normalise(b - 1, s - 2 + STEPS)
                    if s == 3 and not last:
                        prep_rstd(b + 1)
                    if s == 7 and not first:
                        post_rstd(2 * b - 1)
                    if s == 9 and not first:
                        post_final(b - 1, 1 - par, 1)
                    if s in (8, 10) and not last:
                        for i in range(2):
                            prep_low(b + 1, i + (2 if s == 10 else 0))
                    if s == 12 and not last:
                        prep_residuals(b + 1, 1 - par)
                    if s == 5 and first:
                        split_ffn(0, w1_hi[:, :, :].rearrange("p e h -> p (e h)"),
                                  w1_lo[:, :, :].rearrange("p e h -> p (e h)"))
                    if s == 14 and first:
                        split_ffn(1, w2_hi[:, :, :, :].rearrange("p e k d -> p (e k d)"),
                                  w2_lo[:, :, :, :].rearrange("p e k d -> p (e k d)"))
                    if s == 14:
                        post_rstd(2 * b)
                    if s == 15:
                        post_final(b, par, 0)

            bodies(pool, body)
            normalise(LAST, STEPS - 2)
            normalise(LAST, STEPS - 1)
            post_rstd(2 * NB - 1)
            post_final(LAST, LAST % 2, 1)

            def b_rstd(c):
                pool.wait_ge(b_guess_ready, c + 1)
                newton(var_e2, rstd2, newt2, TH, b_newton_step, c, b_rstd_ready)

            def hid_low(c, u):
                pool.wait_ge(hid_hi_ready, E * c + u + 1)
                pool.tensor_tensor(hid_lo[:, u % 4, :, :], hid[:, u % 2, :, :], hid_hi[:, u % 4, :, :],
                                   ALU.subtract).then_inc(hid_lo_ready, 1)

            def body_b(b, par=None):
                for half in range(2):
                    for u in range(E):
                        hid_low(2 * b + half, u)
                        if u == 0 and not (half == 1 and isinstance(b, int) and b == LAST):
                            b_rstd(2 * b + half + 1)

            b_rstd(0)
            bodies(pool, body_b)

        @block.scalar
        def _(act):
            act.wait_ge(w_turned, 1)
            act.activation(wqkv_hi[:], side_tiles(0)[:, 0:3, :], ACT.Copy, scale=WSCALE).then_inc(w_split, 1)
            act.activation(woT[:], side_tiles(0)[:, 3, :], ACT.Copy).then_inc(w_split, 1)
            act.wait_ge(w_turned, 2)
            act.activation(vec[:], side(1)[:, 0:E * KH + 3], ACT.Copy).then_inc(w_split, 1)
            act.activation(bq_scaled[:], side(1)[:, E * KH:E * KH + 1], ACT.Copy, scale=QSCALE).then_inc(w_split, 1)
            act.activation(bv_total[:], side(1)[:, E * KH + 2:E * KH + 3], ACT.Copy, scale=float(T)).then_inc(w_split, 1)

            def xT_high(bb, c):
                act.wait_ge(xT_done, 2 * bb + c + 1)
                act.activation(xT_hi[:, c, :], side(c), ACT.Copy).then_inc(xT_hi_ready, 1)

            def qk_bias(bb, i):
                act.wait_ge(qk_proj_done, 4 * bb + i + 1)
                act.activation(qk[:, i, :], side(i % 2), ACT.Identity,
                               bias=bq_scaled[:] if i < 2 else vec[:, E * KH + 1:E * KH + 2],
                               scale=(QSCALE if i < 2 else 1.0) / WSCALE).then_inc(qk_ready, 1)

            def v_copy(bb, par, c):
                act.wait_ge(v_proj_done, 2 * bb + c + 1)
                act.activation(v_sb[:, par, c * TH:c * TH + TH, :, 0:DH],
                               side_tiles(c).rearrange("p t (h d) -> p t h d", h=HEADS), ACT.Copy,
                               scale=1.0 / WSCALE).then_inc(v_ready, 1)

            def pv_copy(b, s):
                g = STEPS * b + s
                wait(act, ctx_added, g - 1)
                for i in range(2):
                    act.wait_ge(pv_done, 2 * g + i + 1)
                    act.activation(pv_sb[:, s % 2, 2 * i:2 * i + 2, :, :].rearrange("p t h d -> p (t h d)"),
                                   sum_ps[:, i, 0:2 * HEADS * (DH + 1)], ACT.Copy).then_inc(pv_copied, 1)

            def ctxT_out(n):
                act.wait_ge(ctxn_turned, n + 1)
                act.activation(ctxT[:], side(0), ACT.Identity, bias=bv_total[:]).then_inc(ctxT_ready, 1)

            act.wait_ge(w_split, 5)
            for c in range(2):
                xT_high(0, c)
            for i in range(4):
                qk_bias(0, i)
            for c in range(2):
                v_copy(0, 0, c)
            for k in range(T):
                act.wait_ge(mask_turned, k + 1)
                act.activation(limit[:, k, :], side(k % 2).bitcast(BF16), ACT.Copy, bias=-LIMIT).then_inc(limit_ready, 1)

            def exp(b, s):
                for u in range(2):
                    act.wait_ge(clip_done, 2 * STEPS * b + 2 * s + u + 1)
                    wait(act, pv_done, 2 * (STEPS * b + s - 1))
                    act.activation(probs[:, s % 2, 2 * u:2 * u + 2, :], clipped[:, s % 2, 2 * u:2 * u + 2, :],
                                   ACT.Exp).then_inc(exp_done, 1)
                    if u == 0:
                        if s:
                            pv_copy(b, s - 1)
                        elif not (isinstance(b, int) and b == 0):
                            pv_copy(b - 1, STEPS - 1)

            def body(b, par=None):
                par = b % 2 if par is None else par
                first, last = isinstance(b, int) and b == 0, isinstance(b, int) and b == LAST
                for s in range(STEPS):
                    exp(b, s)
                    if s == 3 and not first:
                        ctxT_out(2 * b - 1)
                    if s == 5 and not last:
                        for c in range(2):
                            xT_high(b + 1, c)
                    if s == 7 and not last:
                        for i in range(2):
                            qk_bias(b + 1, i)
                    if s == 9 and not last:
                        for i in range(2, 4):
                            qk_bias(b + 1, i)
                    if s == 11:
                        ctxT_out(2 * b)
                    if s == 14 and not last:
                        for c in range(2):
                            v_copy(b + 1, 1 - par, c)

            bodies(act, body)
            pv_copy(LAST, STEPS - 1)
            ctxT_out(2 * NB - 1)

            def x2T_high(c, par):
                act.wait_ge(x2T_done, c + 1)
                act.activation(x2T_hi[:, par, :], side(0), ACT.Copy).then_inc(x2T_hi_ready, 1)

            def gate_exps(c):
                act.wait_ge(gate_dve, GATE_OPS * c + 3)
                act.activation(logit[:], logit[:], ACT.Exp).then_inc(gate_exp, 1)

            def gelu(c, u):
                n = E * c + u
                for k in range(KH):
                    act.wait_ge(z_done, 2 * n + k + 1)
                    if k == 0:
                        wait(act, hid_lo_ready, n - 1)
                    act.activation(hid[:, u % 2, k, :], score_ps[:, 2 * (u % 2) + k, :], ACT.Gelu,
                                   bias=vec[:, KH * u + k:KH * u + k + 1], scale=1.0 / WSCALE).then_inc(gelu_done, 1)

            def body_b(b, par=None):
                for half in range(2):
                    c = 2 * b + half
                    final = half == 1 and isinstance(b, int) and b == LAST
                    for u in range(E):
                        gelu(c, u)
                        if u == 2 and not final:
                            x2T_high(c + 1, 1 - half)
                        if u == 4 and not final:
                            gate_exps(c + 1)

            x2T_high(0, 0)
            gate_exps(0)
            bodies(act, body_b)

        @block.vector
        def _(dve):
            def rstd_guess(bb, n, st, mean, sq, var_, y, step, done):
                at = STAT_STEPS * bb
                dve.wait_ge(step, at + 1)
                dve.tensor_tensor(mean[:, 0:n], st[:, 0:n, 1], st[:, 0:n, 4], ALU.add)
                dve.tensor_tensor(var_[:, 0:n], st[:, 0:n, 2], st[:, 0:n, 5], ALU.add)
                dve.tensor_tensor(sq[:, 0:n], st[:, 0:n, 1], st[:, 0:n, 4], ALU.subtract).then_inc(step, 1)
                dve.wait_ge(step, at + 2)
                dve.tensor_tensor(sq[:, 0:n], sq[:, 0:n], sq[:, 0:n], ALU.mult).then_inc(step, 1)
                dve.tensor_scalar(mean[:, 0:n], mean[:, 0:n], 0.5, None, ALU.mult)
                dve.wait_ge(step, at + 3)
                dve.scalar_tensor_tensor(out=var_[:, 0:n], in0=sq[:, 0:n], scalar=D / 4.0, in1=var_[:, 0:n],
                                         op0=ALU.mult, op1=ALU.add).then_inc(step, 1)
                dve.wait_ge(step, at + 4)
                dve.tensor_scalar(var_[:, 0:n], var_[:, 0:n], 0.5 / D, 0.5 * EPS, ALU.mult, ALU.add).then_inc(step, 1)
                dve.wait_ge(step, at + 5)
                dve.tensor_scalar(y[:, 0:n].bitcast(I32), var_[:, 0:n].bitcast(I32), 1, None,
                                  ALU.logical_shift_right).then_inc(step, 1)
                dve.wait_ge(step, at + 6)
                dve.tensor_scalar(y[:, 0:n].bitcast(I32), y[:, 0:n].bitcast(I32), -1.0, RSQRT_MAGIC,
                                  ALU.mult, ALU.add).then_inc(done, 1)

            def prep_stats(bb, a, z):
                dve.wait_ge(x_loaded, 16 * (bb + 1))
                for t in range(a, z):
                    ins = dve.bn_stats(stats[:, t, :], xin[:, t, :])
                if z == T:
                    ins.then_inc(norm_step, 1)

            def prep_guess(bb):
                rstd_guess(bb, T, stats, mean, msq, var_e, rstd, norm_step, guess_ready)

            def prep_xn(bb):
                dve.wait_ge(rstd_ready, bb + 1)
                wait(dve, xn_bo_ready, bb)
                for t in range(T):
                    ins = dve.tensor_scalar(xn[:, t, :], xin[:, t, :], mean[:, t:t + 1], rstd[:, t:t + 1],
                                            ALU.subtract, ALU.mult)
                ins.then_inc(xn_ready, 1)

            def xT_low(bb, c):
                dve.wait_ge(xT_hi_ready, 2 * bb + c + 1)
                dve.tensor_tensor(xT_lo[:, c, :], side(c), xT_hi[:, c, :], ALU.subtract).then_inc(xT_lo_ready, 1)

            def qk_high(bb, i):
                dve.wait_ge(qk_ready, 4 * bb + i + 1)
                dve.tensor_copy(qk_hi[:, i, :], qk[:, i, :]).then_inc(qk_hi_ready, 1)

            def clip(b, s):
                for u in range(2):
                    dve.wait_ge(qk_done, 2 * STEPS * b + 2 * s + u + 1)
                    wait(dve, exp_done, 2 * STEPS * b + 2 * s + u - 3)
                    k, half = s % T, s // T
                    dve.scalar_tensor_tensor(
                        out=clipped[:, s % 2, 2 * u:2 * u + 2, :], in0=score_ps[:, 2 * u:2 * u + 2, :], scalar=-LIMIT,
                        in1=limit[:, k:k + 1, half * HALF:half * HALF + HALF].to_broadcast([P, 2, HALF]),
                        op0=ALU.max, op1=ALU.min).then_inc(clip_done, 1)

            def rden_of(b, s):
                g = STEPS * b + s
                dve.wait_ge(pv_copied, 2 * g + 2)
                wait(dve, ctx_added, g - 1)
                dve.reciprocal(rden[:, s % 2, :].rearrange("p (t h) -> p t h", t=TH),
                               pv_sb[:, s % 2, :, :, DH]).then_inc(rden_ready, 1)

            def post_res(n, par, half):
                dve.wait_ge(wo_done, n + 1)
                dve.tensor_tensor(res[:], side_tiles(1), xn_bo[:, par, half * TH:half * TH + TH, :],
                                  ALU.add).then_inc(res_ready, 1)

            def post_stats(n):
                dve.wait_ge(res_ready, n + 1)
                for t in range(TH):
                    ins = dve.bn_stats(stats2[:, t, :], res[:, t, :])
                ins.then_inc(norm2_step, 1)
                rstd_guess(n, TH, stats2, mean2, msq2, var_e2, rstd2, norm2_step, guess2_ready)

            def post_y(n):
                dve.wait_ge(rstd2_ready, n + 1)
                wait(dve, x1_ready, n)
                for t in range(TH):
                    ins = dve.tensor_scalar(y_sb[:, t, :], res[:, t, :], mean2[:, t:t + 1], rstd2[:, t:t + 1],
                                            ALU.subtract, ALU.mult)
                ins.then_inc(y_ready, 1)

            prep_stats(0, 0, T)
            prep_guess(0)
            dve.wait_ge(w_split, 2)
            dve.scalar_tensor_tensor(out=wqkv_lo[:], in0=side_tiles(0)[:, 0:3, :], scalar=WSCALE, in1=wqkv_hi[:],
                                     op0=ALU.mult, op1=ALU.subtract).then_inc(w_low, 1)
            prep_xn(0)
            for c in range(2):
                xT_low(0, c)
            for i in range(4):
                qk_high(0, i)
            for t in range(T):
                dve.wait_ge(adj_loaded[t], 16)
                dve.tensor_scalar(mask20[:, t, :, :], adj_raw[:, t, :].rearrange("p (k q) -> p k q", k=T), 0.0, 2 * LIMIT,
                                  ALU.not_equal, ALU.mult).then_inc(mask_made, 1)

            def body(b, par=None):
                par = b % 2 if par is None else par
                first, last = isinstance(b, int) and b == 0, isinstance(b, int) and b == LAST
                for s in range(STEPS):
                    if first and s < T:
                        dve.wait_ge(limit_ready, s + 1)
                    if first and s == 0:
                        dve.wait_ge(mask_turned, T)
                    clip(b, s)
                    if s >= 2:
                        rden_of(b, s - 2)
                    elif not first:
                        rden_of(b - 1, s - 2 + STEPS)
                    if not last:
                        if s == 0:
                            prep_stats(b + 1, 0, TH)
                        if s == 1:
                            prep_stats(b + 1, TH, T)
                        if s == 3:
                            prep_guess(b + 1)
                        if s == 4:
                            prep_xn(b + 1)
                        if s == 6:
                            for c in range(2):
                                xT_low(b + 1, c)
                        if s in (8, 10):
                            for i in range(2):
                                qk_high(b + 1, i + (2 if s == 10 else 0))
                    if not first:
                        if s == 5:
                            post_res(2 * b - 1, 1 - par, 1)
                        if s == 7:
                            post_stats(2 * b - 1)
                        if s == 9:
                            post_y(2 * b - 1)
                    if s == 13:
                        post_res(2 * b, par, 0)
                    if s == 14:
                        post_stats(2 * b)
                    if s == 15:
                        post_y(2 * b)

            bodies(dve, body)
            n = 2 * NB - 1
            rden_of(LAST, STEPS - 2)
            rden_of(LAST, STEPS - 1)
            post_res(n, LAST % 2, 1)
            post_stats(n)
            post_y(n)

            def x1_half(b, half):
                return x1[:, b, half * HALF:half * HALF + HALF].rearrange("p (t d) -> p t d", t=TH)

            def b_stats(b, half):
                c = 2 * b + half
                for t in range(TH):
                    ins = dve.bn_stats(stats2[:, t, :], x1[:, b, (half * TH + t) * P:(half * TH + t + 1) * P])
                ins.then_inc(b_norm_step, 1)
                rstd_guess(c, TH, stats2, mean2, msq2, var_e2, rstd2, b_norm_step, b_guess_ready)

            def b_xn(b, half):
                c = 2 * b + half
                dve.wait_ge(b_rstd_ready, c + 1)
                for t in range(TH):
                    ins = dve.tensor_scalar(xn2[:, t, :], x1[:, b, (half * TH + t) * P:(half * TH + t + 1) * P],
                                            mean2[:, t:t + 1], rstd2[:, t:t + 1], ALU.subtract, ALU.mult)
                ins.then_inc(xn2_ready, 1)

            def b_low(c, par):
                dve.wait_ge(x2T_hi_ready, c + 1)
                dve.tensor_tensor(x2T_lo[:, par, :], side(0), x2T_hi[:, par, :], ALU.subtract).then_inc(x2T_lo_ready, 1)

            def b_logits(c):
                at = GATE_OPS * c
                dve.wait_ge(gate_done, c + 1)
                dve.scalar_tensor_tensor(out=logit[:], in0=side(1)[:, 0:TH * E].rearrange("p (t e) -> p t e", t=TH),
                                         scalar=1.0 / WSCALE,
                                         in1=gate_b_bc[:, :].rearrange("p (o e) -> p o e", o=1).to_broadcast([P, TH, E]),
                                         op0=ALU.mult, op1=ALU.add).then_inc(gate_dve, 1)
                dve.wait_ge(gate_dve, at + 1)
                dve.tensor_reduce(gsum[:], logit[:], AX.X, ALU.max).then_inc(gate_dve, 1)
                dve.wait_ge(gate_dve, at + 2)
                dve.tensor_tensor(logit[:], logit[:], gsum[:, :].rearrange("p (t o) -> p t o", o=1).to_broadcast([P, TH, E]),
                                  ALU.subtract).then_inc(gate_dve, 1)

            def b_weights(c):
                at = GATE_OPS * c
                dve.wait_ge(gate_exp, c + 1)
                dve.tensor_reduce(gsum[:], logit[:], AX.X, ALU.add).then_inc(gate_dve, 1)
                dve.wait_ge(gate_dve, at + 4)
                dve.reciprocal(gsum[:], gsum[:]).then_inc(gate_dve, 1)
                dve.wait_ge(gate_dve, at + 5)
                dve.tensor_tensor(gprob[:], logit[:], gsum[:, :].rearrange("p (t o) -> p t o", o=1).to_broadcast([P, TH, E]),
                                  ALU.mult).then_inc(gate_dve, 1)
                dve.wait_ge(gate_dve, at + 6)
                dve.tensor_scalar(gprob_s[:], gprob[:], 1.0 / WSCALE, None, ALU.mult)
                for t in range(TH):
                    ins = dve.max(top[:, t, :], gprob[:, t, :])
                ins.then_inc(gate_dve, 1)

            def b_top_known(c):
                dve.wait_ge(gate_dve, GATE_OPS * c + 7)

            def b_picks(c, par):
                at = GATE_OPS * c
                for t in range(TH):
                    ins = dve.max_index(top_at[:, t, :], top[:, t, :], gprob[:, t, :])
                ins.then_inc(gate_dve, 1)
                dve.wait_ge(gate_dve, at + 8)
                dve.tensor_copy(top_no[:], top_at[:, :, 0:2]).then_inc(gate_dve, 1)
                dve.wait_ge(gate_dve, at + 9)
                for j in range(2):
                    ins = dve.tensor_tensor(
                        pick[:, j, :, :], expert_no[:, :].rearrange("p (o e) -> p o e", o=1).to_broadcast([P, TH, E]),
                        top_no[:, :, j:j + 1].to_broadcast([P, TH, E]), ALU.is_equal)
                ins.then_inc(gate_dve, 1)
                dve.wait_ge(gate_dve, at + 10)
                dve.tensor_tensor(pick[:, 0, :, :], pick[:, 0, :, :], pick[:, 1, :, :], ALU.add).then_inc(gate_dve, 1)
                dve.wait_ge(gate_dve, at + 11)
                dve.tensor_tensor(cw_s[:, par, :, :], pick[:, 0, :, :], gprob_s[:], ALU.mult)
                dve.tensor_tensor(cw[:], pick[:, 0, :, :], gprob[:], ALU.mult).then_inc(cw_ready, 1)

            def b_cwT(c):
                dve.wait_ge(cwT_done, c + 1)
                dve.tensor_copy(cwT, side(1)[0:E, :]).then_inc(cwT_ready, 1)

            def b_start(b, half):
                c = 2 * b + half
                dve.wait_ge(b2_done, c + 1)
                wait(dve, stored[half], 16 * b)
                dve.tensor_tensor(acc[:, half, :, :], side_tiles(0), x1_half(b, half), ALU.add).then_inc(acc_start, 1)

            def hid_high(c, u):
                n = E * c + u
                dve.wait_ge(gelu_done, 2 * n + 2)
                wait(dve, y_done, n - 3)
                dve.tensor_copy(hid_hi[:, u % 4, :, :], hid[:, u % 2, :, :]).then_inc(hid_hi_ready, 1)

            def add_up(c, half, u):
                n = E * c + u
                dve.wait_ge(y_done, n + 1)
                if u == 0:
                    dve.wait_ge(acc_start, c + 1)
                else:
                    dve.wait_ge(acc_done, n)
                for t in range(TH):
                    ins = dve.scalar_tensor_tensor(out=acc[:, half, t, :], in0=sum_ps[:, u % 2, t * P:t * P + P],
                                                   scalar=cw_s[:, half, t, u:u + 1], in1=acc[:, half, t, :],
                                                   op0=ALU.mult, op1=ALU.add)
                ins.then_inc(acc_done, 1)

            def body_b(b, par=None):
                for half in range(2):
                    c = 2 * b + half
                    nb, nh = (b, 1) if half == 0 else (b + 1, 0)
                    final = half == 1 and isinstance(b, int) and b == LAST
                    for u in range(E):
                        if u == 6 and not final:
                            b_top_known(c + 1)
                        hid_high(c, u)
                        if not (u == 0 and half == 0 and isinstance(b, int) and b == 0):
                            pc, ph, pu = (c, half, u - 1) if u else (c - 1, 1 - half, E - 1)
                            add_up(pc, ph, pu)
                            if u == 0:
                                b_start(b, half)
                        if final:
                            continue
                        if u == 0:
                            b_stats(nb, nh)
                        if u == 1:
                            b_xn(nb, nh)
                        if u == 3:
                            b_low(c + 1, 1 - half)
                        if u == 4:
                            b_logits(c + 1)
                        if u == 5:
                            b_weights(c + 1)
                        if u == 6:
                            b_picks(c + 1, 1 - half)
                        if u == 7:
                            b_cwT(c + 1)

            dve.wait_ge(x1_ready, 2 * NB)
            dve.wait_ge(exp_done, 2 * STEPS * NB)
            dve.wait_ge(pv_done, 2 * STEPS * NB)
            b_stats(0, 0)
            b_xn(0, 0)
            b_low(0, 0)
            b_logits(0)
            b_weights(0)
            b_top_known(0)
            b_picks(0, 0)
            b_cwT(0)
            b_start(0, 0)
            bodies(dve, body_b)
            add_up(CHUNKS - 1, 1, E - 1)

        @block.tensor
        def _(pe):
            def turn(dst, src, idn):
                return pe.transpose(dst, src, idn)

            def three(dst, a_hi, a_lo, b_hi, b_lo):
                pe.matmul(dst, a_hi, b_hi, start=True, stop=False)
                pe.matmul(dst, a_hi, b_lo, start=False, stop=False)
                return pe.matmul(dst, a_lo, b_hi, start=False, stop=True)

            pe.wait_ge(consts_ready, 4 + E + 2)
            pe.wait_ge(w_loaded, 16 * 8)
            for i in range(4):
                ins = turn(side_tiles(0)[:, i, :], wqkvo_raw[:, i, :], ident[:])
            ins.then_inc(w_turned, 1)
            pe.matmul(side(1)[:, 0:E * KH + 3], vec_raw[:], ident[0:E * KH + 3, 0:E * KH + 3],
                      start=True, stop=True).then_inc(w_turned, 1)

            def xT(bb):
                pe.wait_ge(xn_ready, bb + 1)
                for c in range(2):
                    for t in range(TH):
                        ins = turn(side_tiles(c)[:, t, :], xn[:, c * TH + t, :], ident[:])
                    ins.then_inc(xT_done, 1)

            def qk_proj(bb, i):
                c = i % 2
                pe.wait_ge(xT_lo_ready, 2 * bb + c + 1)
                three(side(c), wqkv_hi[:, i // 2, :], wqkv_lo[:, i // 2, :], xT_hi[:, c, :],
                      xT_lo[:, c, :]).then_inc(qk_proj_done, 1)

            def v_proj(bb, c):
                for t in range(TH):
                    ins = three(side_tiles(c)[:, t, :], xT_hi[:, c, t * P:t * P + P], xT_lo[:, c, t * P:t * P + P],
                                wqkv_hi[:, 2, :], wqkv_lo[:, 2, :])
                ins.then_inc(v_proj_done, 1)

            def scores(b, par, s):
                k, half = s % T, s // T
                if s == 0:
                    pe.wait_ge(stacked, 16 * STACKS * (b + 1))
                for u in range(2):
                    wait(pe, clip_done, 2 * STEPS * b + 2 * s + u - 1)
                    for h in (2 * u, 2 * u + 1):
                        ins = pe.matmul(score_ps[:, h, :], kstack[:, par, h, k * P:k * P + P],
                                        qstack[:, par, h, half * HALF:half * HALF + HALF], start=True, stop=True)
                    ins.then_inc(qk_done, 1)

            def sums(b, par, s):
                k, g = s % T, STEPS * b + s
                if s == 0:
                    pe.wait_ge(v_ready, 2 * b + 2)
                pe.wait_ge(exp_done, 2 * g + 2)
                for i in range(2):
                    wait(pe, pv_copied, 2 * g - 1 + i)
                    for t in range(2):
                        for h in range(HEADS):
                            at = (t * HEADS + h) * (DH + 1)
                            ins = pe.matmul(sum_ps[:, i, at:at + DH + 1],
                                            probs[:, s % 2, h, (2 * i + t) * P:(2 * i + t) * P + P],
                                            v_sb[:, par, k, h, :], start=True, stop=True)
                    ins.then_inc(pv_done, 1)

            def ctxn_turn(n, n_par):
                pe.wait_ge(ctx_added, T * (n + 1))
                for t in range(TH):
                    ins = turn(side_tiles(0)[:, t, :], ctxn[:, n_par, t, :], ident[:])
                ins.then_inc(ctxn_turned, 1)

            def wo(n):
                pe.wait_ge(ctxT_ready, n + 1)
                for t in range(TH):
                    ins = pe.matmul(side_tiles(1)[:, t, :], ctxT[:, t * P:t * P + P], woT[:], start=True, stop=True)
                ins.then_inc(wo_done, 1)

            pe.wait_ge(w_split, 5)
            pe.wait_ge(w_low, 1)
            xT(0)
            for i in range(4):
                if i >= 2:
                    pe.wait_ge(qk_ready, i - 1)
                qk_proj(0, i)
            for c in range(2):
                pe.wait_ge(qk_ready, 3 + c)
                v_proj(0, c)
            pe.wait_ge(mask_made, T)
            for k in range(T):
                if k < 2:
                    pe.wait_ge(v_ready, k + 1)
                else:
                    pe.wait_ge(limit_ready, k - 1)
                for t in range(T):
                    ins = turn(side(k % 2).bitcast(BF16)[:, t * P:t * P + P], mask20[:, t, k, :], identb[:])
                ins.then_inc(mask_turned, 1)
            scores(0, 0, 0)

            def body(b, par=None):
                par = b % 2 if par is None else par
                first, last = isinstance(b, int) and b == 0, isinstance(b, int) and b == LAST
                m, n, bb = 2 * b - 1, 2 * b, b + 1
                for s in range(STEPS):
                    if s + 1 < STEPS:
                        scores(b, par, s + 1)
                    elif not last:
                        scores(b + 1, 1 - par, 0)
                    if s == 3 and not first:
                        pe.wait_ge(v_ready, 2 * b + 2)
                        ctxn_turn(m, 1)
                    if s == 4 and not first:
                        wo(m)
                    if s == 5 and not last:
                        if first:
                            pe.wait_ge(limit_ready, T)
                        else:
                            pe.wait_ge(ctxT_ready, m + 1)
                            pe.wait_ge(res_ready, m + 1)
                        xT(bb)
                    if s == 7 and not last:
                        qk_proj(bb, 0)
                        qk_proj(bb, 1)
                    if s == 9 and not last:
                        pe.wait_ge(qk_ready, 4 * bb + 2)
                        qk_proj(bb, 2)
                        qk_proj(bb, 3)
                    if s == 11:
                        if last:
                            pe.wait_ge(res_ready, m + 1)
                        else:
                            pe.wait_ge(qk_ready, 4 * bb + 3)
                        ctxn_turn(n, 0)
                    if s == 12:
                        if not last:
                            pe.wait_ge(qk_ready, 4 * bb + 4)
                        wo(n)
                    if s == 14 and not last:
                        pe.wait_ge(ctxT_ready, n + 1)
                        v_proj(bb, 0)
                        pe.wait_ge(res_ready, n + 1)
                        v_proj(bb, 1)
                    sums(b, par, s)

            bodies(pe, body)
            n = 2 * NB - 1
            pe.wait_ge(res_ready, n)
            ctxn_turn(n, 1)
            wo(n)

            def x2T(c):
                pe.wait_ge(xn2_ready, c + 1)
                wait(pe, acc_start, c)
                for t in range(TH):
                    ins = turn(side_tiles(0)[:, t, :], xn2[:, t, :], ident[:])
                ins.then_inc(x2T_done, 1)

            def gate(c, par):
                pe.wait_ge(x2T_lo_ready, c + 1)
                wait(pe, cwT_ready, c)
                for t in range(TH):
                    ins = three(side(1)[:, t * E:t * E + E], x2T_hi[:, par, t * P:t * P + P],
                                x2T_lo[:, par, t * P:t * P + P], gate_hi[:], gate_lo[:])
                ins.then_inc(gate_done, 1)

            def turn_cw(c):
                pe.wait_ge(cw_ready, c + 1)
                for t in range(TH):
                    ins = pe.matmul(side(1)[0:E, t * P:t * P + P], cw[:, t, :], ident[:], start=True, stop=True)
                ins.then_inc(cwT_done, 1)

            def weighted_b2(c):
                pe.wait_ge(cwT_ready, c + 1)
                for t in range(TH):
                    ins = pe.matmul(side_tiles(0)[:, t, :], cwT[:, t * P:t * P + P], b2_sb[:], start=True, stop=True)
                ins.then_inc(b2_done, 1)

            def hidden(c, par, u):
                n = E * c + u
                if u == 0:
                    pe.wait_ge(x2T_lo_ready, c + 1)
                wait(pe, gelu_done, 2 * n - 2)
                for k in range(KH):
                    three(score_ps[:, 2 * (u % 2) + k, :], w1_hi[:, u, k * P:k * P + P], w1_lo[:, u, k * P:k * P + P],
                          x2T_hi[:, par, :], x2T_lo[:, par, :]).then_inc(z_done, 1)

            def second(c, u):
                n = E * c + u
                pe.wait_ge(hid_lo_ready, n + 1)
                wait(pe, acc_done, n - 1)
                for t in range(TH):
                    for k in range(KH):
                        cols = slice(t * P, t * P + P)
                        hi, lo = hid_hi[:, u % 4, k, cols], hid_lo[:, u % 4, k, cols]
                        dst = sum_ps[:, u % 2, cols]
                        pe.matmul(dst, hi, w2_hi[:, u, k, :], start=(k == 0), stop=False)
                        pe.matmul(dst, hi, w2_lo[:, u, k, :], start=False, stop=False)
                        ins = pe.matmul(dst, lo, w2_hi[:, u, k, :], start=False, stop=(k == KH - 1))
                ins.then_inc(y_done, 1)

            pe.wait_ge(res_ready, 2 * NB)
            pe.wait_ge(gate_step, 3)
            pe.wait_ge(ffn_step, 6)
            x2T(0)
            gate(0, 0)
            hidden(0, 0, 0)
            hidden(0, 0, 1)
            turn_cw(0)
            weighted_b2(0)

            def body_b(b, par=None):
                for half in range(2):
                    c = 2 * b + half
                    final = half == 1 and isinstance(b, int) and b == LAST
                    for u in range(E):
                        if u + 2 < E:
                            hidden(c, half, u + 2)
                        elif not final:
                            hidden(c + 1, 1 - half, u + 2 - E)
                        if u == 0 and not (half == 0 and isinstance(b, int) and b == 0):
                            weighted_b2(c)
                        if not final:
                            if u == 2:
                                x2T(c + 1)
                            if u == 4:
                                gate(c + 1, 1 - half)
                            if u == 7:
                                turn_cw(c + 1)
                        second(c, u)

            bodies(pe, body_b)


_INS = ["x", "adj", "L0_gnn_Wq", "L0_gnn_bq", "L0_gnn_Wk", "L0_gnn_bk", "L0_gnn_Wv", "L0_gnn_bv", "L0_gnn_Wo",
        "L0_gnn_bo", "L0_gnn_gamma", "L0_gnn_beta", "L0_ffn_gate_w", "L0_ffn_gate_b", "L0_ffn_W1", "L0_ffn_b1",
        "L0_ffn_W2", "L0_ffn_b2"]


def kernel(**inputs):
    import numpy as np
    import concourse.bacc as bacc
    from concourse.bass_utils import run_bass_kernel_spmd

    nc = bacc.Bacc("TRN2", target_bir_lowering=False, num_devices=1)
    arrays, args = {}, []
    for name in _INS:
        a = np.ascontiguousarray(inputs[name])
        arrays[f"in_{name}"] = a
        args.append(nc.dram_tensor(f"in_{name}", a.shape, mybir.dt.from_np(a.dtype), kind="ExternalInput").ap())
    out = nc.dram_tensor("out_x", inputs["x"].shape, F32, kind="ExternalOutput").ap()
    gnn_moe(nc, *args, out)
    r = run_bass_kernel_spmd(nc, [arrays], core_ids=[0])
    return r.results[0]["out_x"]
```

```python
from contextlib import ExitStack

import concourse.bass as bass
from concourse import mybir

ALU = mybir.AluOpType
ACT = mybir.ActivationFunctionType
AX = mybir.AxisListType
F32 = mybir.dt.float32
F16 = mybir.dt.float16
BF16 = mybir.dt.bfloat16
I32 = mybir.dt.int32
U32 = mybir.dt.uint32

P = 128
WSCALE = 256.0
EPS = 1e-5
LIMIT = 10.0
RSQRT_MAGIC = float(0x5F3759DF - 0x400000)
NEWTON = 3
NEWTON_OPS = 4 * NEWTON
STAT_STEPS = 6


def gnn_moe(nc, x, adj, Wq, bq, Wk, bk, Wv, bv, Wo, bo, gamma, beta, gate_w, gate_b, W1, b1, W2, b2, out):
    NB, N, D = x.shape
    T = N // P
    HEADS, DH = 4, 32
    E, _, HID = W1.shape
    KH = HID // P
    HALF = N // 2
    TH = T // 2
    STEPS = 2 * T
    STACKS = 8
    GROUP = 4
    GROUPS = STEPS // GROUP
    RING = 2 * GROUP
    LAG = GROUP + 3
    assert D == P and HEADS * DH == D and N == 1024 and HALF == 512 and KH == 2 and E == 8
    QSCALE = float(DH) ** -0.5

    ctx = ExitStack()
    with ctx:
        def sb(name, shape, dt):
            return ctx.enter_context(nc.sbuf_tensor(name, shape, dt))

        def sem(name):
            return ctx.enter_context(nc.semaphore(name))

        ident = sb("ident", [P, P], F32)
        identb = sb("identb", [P, P], BF16)
        three_halves = sb("three_halves", [P, T], F32)
        expert_no = sb("expert_no", [P, E], F32)
        vec_raw = sb("vec_raw", [E * KH + 3, P], F32)
        vec = sb("vec", [P, E * KH + 3], F32)
        bq_scaled = sb("bq_scaled", [P, 1], F32)
        bv_total = sb("bv_total", [P, 1], F32)
        wqkv_hi = sb("wqkv_hi", [P, 3, P], F16)
        wqkv_lo = sb("wqkv_lo", [P, 3, P], F16)
        woT = sb("woT", [P, P], F32)
        rows_bc = sb("rows_bc", [P, 3, P], F32)
        gate_b_bc = sb("gate_b_bc", [P, E], F32)
        gate_raw = sb("gate_raw", [P, E], F32)
        gate_hi = sb("gate_hi", [P, E], F16)
        gate_lo = sb("gate_lo", [P, E], F16)
        w1_hi = sb("w1_hi", [P, E, HID], F16)
        w1_lo = sb("w1_lo", [P, E, HID], F16)
        w2_hi = sb("w2_hi", [P, E, KH, P], F16)
        w2_lo = sb("w2_lo", [P, E, KH, P], F16)
        b2_sb = sb("b2_sb", [E, P], F32)
        limit = sb("limit", [P, T, N], BF16)
        x1 = sb("x1", [P, NB, T * P], F32)
        ctx_sb = sb("ctx_sb", [P, RING, HALF], F32)
        adj_raw = [x1[:, t + 1, :].bitcast(I32) for t in range(T - 1)] + \
            [ctx_sb[:, 0:2, :].rearrange("p r n -> p (r n)").bitcast(I32)]
        w_raw = [x1[:, NB - 4 + 2 * i:NB - 2 + 2 * i, :].rearrange("p b n -> p (b n)") for i in range(2)]
        xn = sb("xn", [P, T, P], F32)
        xn_bo = sb("xn_bo", [P, 2, T, P], F32)
        xT_hi = sb("xT_hi", [P, 2, HALF], F16)
        xT_lo = sb("xT_lo", [P, 2, HALF], F16)
        qk = sb("qk", [P, 4, HALF], F32)
        qk_hi = sb("qk_hi", [P, 4, HALF], F16)
        qk_lo = sb("qk_lo", [P, 4, HALF], F16)
        qstack = sb("qstack", [P, 2, HEADS, N], F16)
        kstack = sb("kstack", [P, 2, HEADS, N], F16)
        v_sb = sb("v_sb", [P, 2, T, P], F32)
        gather = sb("gather", [P, 2, GROUP, DH], F32)
        clip_buf = sb("clip_buf", [P, 2 * HEADS * HALF], F32)
        prob_buf = sb("prob_buf", [P, 2 * HEADS * HALF], F32)
        clipped = clip_buf[:, :].rearrange("p (r h n) -> p r h n", r=2, h=HEADS)
        probs = prob_buf[:, :].rearrange("p (r h n) -> p r h n", r=2, h=HEADS)
        mask20 = clip_buf[:, :].bitcast(BF16).rearrange("p (t k q) -> p t k q", t=T, k=T)
        rinv = sb("rinv", [P, HALF // 2], F32)
        rspread = sb("rspread", [P, GROUP, HALF], F32)
        ctx_acc = sb("ctx_acc", [P, HALF], F32)
        ctxT = sb("ctxT", [P, HALF], F32)
        res = sb("res", [P, TH, P], F32)
        wqkvo_raw = res
        stats = sb("stats", [P, T, 6], F32)
        mean = sb("mean", [P, T], F32)
        shift = sb("shift", [P, T], F32)
        shift2 = sb("shift2", [P, TH], F32)
        msq = sb("msq", [P, T], F32)
        var_e = sb("var_e", [P, T], F32)
        rstd = sb("rstd", [P, T], F32)
        newt = sb("newt", [P, T], F32)
        stats2 = sb("stats2", [P, TH, 6], F32)
        mean2 = sb("mean2", [P, TH], F32)
        msq2 = sb("msq2", [P, TH], F32)
        var_e2 = sb("var_e2", [P, TH], F32)
        rstd2 = sb("rstd2", [P, TH], F32)
        newt2 = sb("newt2", [P, TH], F32)
        hid = ctx_sb[:, :, :].rearrange("p (r k) n -> p r k n", k=KH)
        acc = clip_buf[:, 0:2 * HALF].rearrange("p (r t d) -> p r t d", r=2, t=TH)
        hid_hi = prob_buf[:, 0:2 * KH * HALF].bitcast(F16).rearrange("p (r k n) -> p r k n", r=4, k=KH)
        hid_lo = prob_buf[:, 2 * KH * HALF:4 * KH * HALF].bitcast(F16).rearrange("p (r k n) -> p r k n", r=4, k=KH)
        xn2 = clip_buf[:, 2 * HALF:3 * HALF].rearrange("p (t d) -> p t d", t=TH)
        x2T_hi = qk[:, 0:2, :].rearrange("p a n -> p (a n)").bitcast(F16)[:, 0:2 * HALF].rearrange("p (r n) -> p r n", r=2)
        x2T_lo = qk[:, 2:4, :].rearrange("p a n -> p (a n)").bitcast(F16)[:, 0:2 * HALF].rearrange("p (r n) -> p r n", r=2)
        logit = sb("logit", [P, TH, E], F32)
        top = sb("top", [P, TH, 8], F32)
        top_at = sb("top_at", [P, TH, 8], U32)
        top_no = sb("top_no", [P, TH, 2], F32)
        gsum = sb("gsum", [P, TH], F32)
        gprob = sb("gprob", [P, TH, E], F32)
        gprob_s = sb("gprob_s", [P, TH, E], F32)
        pick = sb("pick", [P, 2, TH, E], F32)
        cw = sb("cw", [P, TH, E], F32)
        cw_s = sb("cw_s", [P, 2, TH, E], F32)
        cwT = rspread[0:E, 0, :]

        score_ps = ctx.enter_context(nc.psum_tensor("score_ps", [P, 4, HALF], F32))
        sum_ps = ctx.enter_context(nc.psum_tensor("sum_ps", [P, 2, HALF], F32))
        side_ps = ctx.enter_context(nc.psum_tensor("side_ps", [P, 2, HALF], F32))
        den_ps = side_ps[:, 1, 0:HALF // 2]

        qk_dram = nc.dram_tensor("qk_dram", (4, P, N), F16, kind="Internal").ap()
        den_dram = nc.dram_tensor("den_dram", (2, P, HALF // 2), F32, kind="Internal").ap()

        def side(i):
            return side_ps[:, i, :]

        def side_tiles(i):
            return side_ps[:, i, :].rearrange("p (t d) -> p t d", t=TH)

        consts_ready = sem("consts_ready")
        w_loaded = sem("w_loaded")
        rows_loaded = sem("rows_loaded")
        adj_loaded = [sem(f"adj_loaded{t}") for t in range(T)]
        ffn_w_loaded = sem("ffn_w_loaded")
        w_turned = sem("w_turned")
        w_split = sem("w_split")
        w_low = sem("w_low")
        mask_made = sem("mask_made")
        mask_turned = sem("mask_turned")
        limit_ready = sem("limit_ready")
        ffn_step = sem("ffn_step")
        gate_step = sem("gate_step")
        x_loaded = sem("x_loaded")
        norm_step = sem("norm_step")
        guess_ready = sem("guess_ready")
        newton_step = sem("newton_step")
        rstd_ready = sem("rstd_ready")
        shift_ready = sem("shift_ready")
        shift2_ready = sem("shift2_ready")
        xn_ready = sem("xn_ready")
        xT_done = sem("xT_done")
        xT_hi_ready = sem("xT_hi_ready")
        xT_lo_ready = sem("xT_lo_ready")
        qk_proj_done = sem("qk_proj_done")
        qk_ready = sem("qk_ready")
        qk_hi_ready = sem("qk_hi_ready")
        qk_lo_ready = sem("qk_lo_ready")
        parts_stored = sem("parts_stored")
        stacked = sem("stacked")
        v_proj_done = sem("v_proj_done")
        v_ready = sem("v_ready")
        x_beta_ready = sem("x_beta_ready")
        xn_bo_ready = sem("xn_bo_ready")
        qk_done = sem("qk_done")
        clip_done = sem("clip_done")
        exp_done = sem("exp_done")
        ctx_done = sem("ctx_done")
        den_added = sem("den_added")
        ctx_copied = sem("ctx_copied")
        rinv_ready = sem("rinv_ready")
        rinv_stored = sem("rinv_stored")
        rspread_loaded = [sem(f"rspread_loaded{j}") for j in range(GROUP)]
        scaled_ready = sem("scaled_ready")
        chunk_added = sem("chunk_added")
        ctxT_ready = sem("ctxT_ready")
        wo_done = sem("wo_done")
        res_ready = sem("res_ready")
        norm2_step = sem("norm2_step")
        guess2_ready = sem("guess2_ready")
        newton2_step = sem("newton2_step")
        rstd2_ready = sem("rstd2_ready")
        y_ready = sem("y_ready")
        y_scaled = sem("y_scaled")
        x1_ready = sem("x1_ready")
        b_norm_step = sem("b_norm_step")
        b_guess_ready = sem("b_guess_ready")
        b_newton_step = sem("b_newton_step")
        b_rstd_ready = sem("b_rstd_ready")
        xn2_ready = sem("xn2_ready")
        x2T_done = sem("x2T_done")
        x2T_hi_ready = sem("x2T_hi_ready")
        x2T_lo_ready = sem("x2T_lo_ready")
        gate_done = sem("gate_done")
        gate_dve = sem("gate_dve")
        gate_exp = sem("gate_exp")
        cw_ready = sem("cw_ready")
        cwT_done = sem("cwT_done")
        cwT_ready = sem("cwT_ready")
        b2_done = sem("b2_done")
        acc_start = sem("acc_start")
        z_done = sem("z_done")
        gelu_done = sem("gelu_done")
        hid_hi_ready = sem("hid_hi_ready")
        hid_lo_ready = sem("hid_lo_ready")
        y_done = sem("y_done")
        acc_done = sem("acc_done")
        stored = [sem(f"stored{i}") for i in range(2)]
        GATE_OPS = 11
        LAST = NB - 1
        CONSTS = 4 + E + 2 * GROUP + 2
        CHUNKS = 2 * NB

        def wait(eng, s, value):
            if not isinstance(value, int) or value > 0:
                eng.wait_ge(s, value)

        def bodies(eng, body):
            body(0)
            with eng.Fori(0, (NB - 2) // 2) as i:
                body(2 * i + 1, 1)
                body(2 * i + 2, 0)
            body(LAST)

        x_v = x.rearrange("b (t p) d -> b p t d", t=T)
        out_v = out.rearrange("b (c t p) d -> b c p t d", c=2, t=TH)

        def x1_tiles(b):
            return x1[:, b, :].rearrange("p (t d) -> p t d", t=T)

        block = ctx.enter_context(nc.Block())

        @block.sync
        def _(sp):
            sp.dma_start(x1_tiles(0), x_v[0]).then_inc(x_loaded, 16)
            for i, w in enumerate((Wq, Wk, Wv, Wo)):
                sp.dma_start(wqkvo_raw[:, i, :], w).then_inc(w_loaded, 16)
            sp.dma_start(vec_raw[0:E * KH, :], b1.rearrange("e (k p) -> (e k) p", p=P)).then_inc(w_loaded, 16)
            for i, v in enumerate((bq, bk, bv)):
                sp.dma_start(vec_raw[E * KH + i:E * KH + i + 1, :], v.rearrange("(o d) -> o d", o=1)).then_inc(w_loaded, 16)
            adj_v = adj.rearrange("(t p) k -> p t k", t=T)
            for t in range(T):
                sp.dma_start(adj_raw[t], adj_v[:, t, :]).then_inc(adj_loaded[t], 16)
            for i, v in enumerate((bo, gamma, beta)):
                sp.dma_start(rows_bc[:, i, :], v.partition_broadcast(P)).then_inc(rows_loaded, 16)
            sp.dma_start(gate_b_bc[:], gate_b.partition_broadcast(P)).then_inc(rows_loaded, 16)
            sp.dma_start(gate_raw[:], gate_w).then_inc(rows_loaded, 16)
            sp.dma_start(b2_sb[:], b2).then_inc(rows_loaded, 16)
            sp.wait_ge(mask_made, T)
            sp.dma_start(w_raw[0].rearrange("p (e h) -> p e h", e=E),
                         W1.rearrange("e d h -> d e h")).then_inc(ffn_w_loaded, 16)
            sp.dma_start(w_raw[1].rearrange("p (e k d) -> p e k d", e=E, k=KH),
                         W2.rearrange("e (k p) d -> p e k d", p=P)).then_inc(ffn_w_loaded, 16)

            def stack(bb, par, first, dst, order):
                if first == 0:
                    wait(sp, qk_done, 2 * STEPS * (bb - 1))
                sp.wait_ge(qk_hi_ready, 4 * bb + first + 2)
                sp.dma_start(qk_dram[first].rearrange("p (c n) -> p c n", c=2),
                             qk_hi[:, first:first + 2, :]).then_inc(parts_stored, 16)
                sp.wait_ge(qk_lo_ready, 4 * bb + first + 2)
                sp.dma_start(qk_dram[first + 1].rearrange("p (c n) -> p c n", c=2),
                             qk_lo[:, first:first + 2, :]).then_inc(parts_stored, 16)
                sp.wait_ge(parts_stored, 64 * bb + 16 * first + 32)
                for r, part in enumerate(order):
                    sp.dma_start(dst[DH * r:DH * r + DH, par, :, :],
                                 qk_dram[first + part].rearrange("(h d) n -> d h n", h=HEADS)).then_inc(stacked, 16)

            def stack_q(bb, par):
                stack(bb, par, 0, qstack, (0, 0, 1, 1))

            def stack_k(bb, par):
                stack(bb, par, 2, kstack, (0, 1, 0, 1))

            def spread(b, i):
                G = GROUPS * b + i
                sp.wait_ge(rinv_ready, G + 1)
                wait(sp, chunk_added, GROUP * G - GROUP + 1)
                sp.dma_start(den_dram[i % 2], rinv[:]).then_inc(rinv_stored, 16)
                sp.wait_ge(rinv_stored, 16 * G + 16)
                rows = den_dram[i % 2].rearrange("(h c j) q -> c j h q", h=HEADS, c=2)
                for j in range(GROUP):
                    if j:
                        wait(sp, chunk_added, GROUP * G - GROUP + j + 1)
                    for c in range(2):
                        sp.dma_start(rspread[:, j, c * (HALF // 2):(c + 1) * (HALF // 2)],
                                     rows[c, j].rearrange("h (o q) -> h o q", o=1).to_broadcast([HEADS, DH, HALF // 2])
                                     ).then_inc(rspread_loaded[j], 16)

            stack_q(0, 0)
            stack_k(0, 0)

            def body(b, par=None):
                par = b % 2 if par is None else par
                first, last = isinstance(b, int) and b == 0, isinstance(b, int) and b == LAST
                if not last:
                    dst, src = x1_tiles(b + 1), x_v[b + 1]
                    if not first:
                        sp.wait_ge(ffn_step, 6)
                    sp.dma_start(dst, src).then_inc(x_loaded, 16)
                if not first:
                    spread(b - 1, GROUPS - 1)
                spread(b, 0)
                spread(b, 1)
                if not last:
                    stack_q(b + 1, 1 - par)
                    stack_k(b + 1, 1 - par)
                spread(b, 2)

            bodies(sp, body)
            spread(LAST, GROUPS - 1)

            def store(b, half):
                sp.wait_ge(acc_done, E * (2 * b + half + 1))
                sp.dma_start(out_v[b, half], acc[:, half, :, :]).then_inc(stored[half], 16)

            with sp.Fori(0, NB) as b:
                store(b, 0)
                store(b, 1)
            sp.wait_ge(stored[0], 16 * NB)
            sp.wait_ge(stored[1], 16 * NB)

        @block.gpsimd
        def _(pool):
            pool.memset(ident[:], 0.0).then_inc(consts_ready, 1)
            pool.memset(identb[:], 0.0).then_inc(consts_ready, 1)
            pool.memset(gather[:], 0.0).then_inc(consts_ready, 1)
            pool.memset(three_halves[:], 1.5).then_inc(consts_ready, 1)
            pool.memset(mean2[:], 0.0).then_inc(x1_ready, 1)
            for e in range(E):
                pool.memset(expert_no[:, e:e + 1], float(e)).then_inc(consts_ready, 1)
            pool.wait_ge(consts_ready, 3)
            for c in range(2):
                for j in range(GROUP):
                    pool.memset(gather[:, c, j, (DH // 2) * c + j:(DH // 2) * (c + 1):GROUP], 1.0).then_inc(consts_ready, 1)
            for m in (ident, identb):
                pool.affine_select(out=m[:], in_=m[:], compare_op=ALU.not_equal, fill=1.0, base=0,
                                   pattern=[[-1, P]], channel_multiplier=1).then_inc(consts_ready, 1)

            def newton(v, y, t, n, step, at, done):
                for i in range(NEWTON):
                    ops = [lambda: pool.tensor_tensor(t[:, 0:n], y[:, 0:n], y[:, 0:n], ALU.mult),
                           lambda: pool.tensor_tensor(t[:, 0:n], t[:, 0:n], v[:, 0:n], ALU.mult),
                           lambda: pool.tensor_tensor(t[:, 0:n], three_halves[:, 0:n], t[:, 0:n], ALU.subtract),
                           lambda: pool.tensor_tensor(y[:, 0:n], y[:, 0:n], t[:, 0:n], ALU.mult)]
                    for k, op in enumerate(ops):
                        j = 4 * i + k
                        if j:
                            pool.wait_ge(step, (NEWTON_OPS - 1) * at + j)
                        if j == NEWTON_OPS - 1:
                            op().then_inc(done, 1)
                        else:
                            op().then_inc(step, 1)

            def prep_rstd(bb):
                pool.wait_ge(guess_ready, bb + 1)
                newton(var_e, rstd, newt, T, newton_step, bb, rstd_ready)
                pool.wait_ge(rstd_ready, bb + 1)
                pool.tensor_tensor(shift[:], mean[:], rstd[:], ALU.mult).then_inc(shift_ready, 1)

            def prep_low(bb, i):
                pool.wait_ge(qk_hi_ready, 4 * bb + i + 1)
                pool.tensor_tensor(qk_lo[:, i, :], qk[:, i, :], qk_hi[:, i, :], ALU.subtract).then_inc(qk_lo_ready, 1)

            def prep_x_beta(bb):
                pool.wait_ge(xn_ready, 2 * bb + 2)
                pool.tensor_tensor(x1_tiles(bb), x1_tiles(bb), rows_bc[:, 2:3, :].to_broadcast([P, T, P]),
                                   ALU.add).then_inc(x_beta_ready, 1)

            def prep_xn_bo(bb, par):
                wait(pool, res_ready, 2 * (bb - 1))
                pool.tensor_tensor(xn_bo[:, par, :, :], xn[:], rows_bc[:, 0:1, :].to_broadcast([P, T, P]),
                                   ALU.add).then_inc(xn_bo_ready, 1)

            def normalise(b, s):
                g, k, half = STEPS * b + s, s % T, s // T
                n = 2 * b + half
                pool.wait_ge(ctx_copied, g + 1)
                pool.wait_ge(rspread_loaded[s % GROUP], 32 * (GROUPS * b + s // GROUP + 1))
                fresh, by = ctx_sb[:, s % RING, :], rspread[:, s % GROUP, :]
                if k == 0:
                    wait(pool, ctxT_ready, n)
                    pool.tensor_tensor(ctx_acc[:], fresh, by, ALU.mult).then_inc(chunk_added, 1)
                else:
                    pool.wait_ge(chunk_added, g)
                    pool.tensor_tensor(fresh, fresh, by, ALU.mult).then_inc(scaled_ready, 1)
                    pool.wait_ge(scaled_ready, (T - 1) * n + k)
                    pool.tensor_tensor(ctx_acc[:], ctx_acc[:], fresh, ALU.add).then_inc(chunk_added, 1)

            def post_rstd(n):
                pool.wait_ge(guess2_ready, n + 1)
                newton(var_e2, rstd2, newt2, TH, newton2_step, n, rstd2_ready)
                pool.wait_ge(rstd2_ready, n + 1)
                pool.tensor_tensor(shift2[:], mean2[:], rstd2[:], ALU.mult).then_inc(shift2_ready, 1)

            def post_final(b, half):
                n = 2 * b + half
                pool.wait_ge(y_ready, n + 1)
                pool.tensor_tensor(res[:], res[:], rows_bc[:, 1:2, :].to_broadcast([P, TH, P]),
                                   ALU.mult).then_inc(y_scaled, 1)
                pool.wait_ge(y_scaled, n + 1)
                pool.wait_ge(x_beta_ready, b + 1)
                x1_half = x1[:, b, half * HALF:half * HALF + HALF].rearrange("p (t d) -> p t d", t=TH)
                pool.tensor_tensor(x1_half, res[:], x1_half, ALU.add).then_inc(x1_ready, 1)

            pool.wait_ge(rows_loaded, 16 * 6)
            prep_rstd(0)
            for i in range(4):
                prep_low(0, i)
            prep_x_beta(0)
            prep_xn_bo(0, 0)
            pool.tensor_scalar(gate_raw[:], gate_raw[:], WSCALE, 1.0, ALU.mult, ALU.mult).then_inc(gate_step, 1)
            pool.wait_ge(gate_step, 1)
            pool.tensor_scalar(gate_hi[:], gate_raw[:], 1.0, 1.0, ALU.mult, ALU.mult).then_inc(gate_step, 1)
            pool.wait_ge(gate_step, 2)
            pool.tensor_tensor(gate_lo[:], gate_raw[:], gate_hi[:], ALU.subtract).then_inc(gate_step, 1)

            def split_ffn(n, hi, lo):
                pool.wait_ge(ffn_w_loaded, 16 * 2)
                pool.tensor_scalar(w_raw[n], w_raw[n], WSCALE, 1.0, ALU.mult, ALU.mult).then_inc(ffn_step, 1)
                pool.wait_ge(ffn_step, 3 * n + 1)
                pool.tensor_scalar(hi, w_raw[n], 1.0, 1.0, ALU.mult, ALU.mult).then_inc(ffn_step, 1)
                pool.wait_ge(ffn_step, 3 * n + 2)
                pool.tensor_tensor(lo, w_raw[n], hi, ALU.subtract).then_inc(ffn_step, 1)

            def body(b, par=None):
                par = b % 2 if par is None else par
                first, last = isinstance(b, int) and b == 0, isinstance(b, int) and b == LAST
                for s in range(STEPS):
                    if s == 2 and not last:
                        prep_rstd(b + 1)
                    if s == 4 and not first:
                        post_rstd(2 * b - 2)
                    if s == 12 and not first:
                        post_rstd(2 * b - 1)
                    if s >= LAG:
                        normalise(b, s - LAG)
                    elif not first:
                        normalise(b - 1, s - LAG + STEPS)
                    if s == 7 and not first:
                        post_final(b - 1, 0)
                    if s == 15 and not first:
                        post_final(b - 1, 1)
                    if s in LOW_AT and not last:
                        prep_low(b + 1, LOW_AT.index(s))
                    if s == 5 and not last:
                        prep_x_beta(b + 1)
                    if s == 13 and not last:
                        prep_xn_bo(b + 1, 1 - par)
                    if s == 5 and first:
                        split_ffn(0, w1_hi[:, :, :].rearrange("p e h -> p (e h)"),
                                  w1_lo[:, :, :].rearrange("p e h -> p (e h)"))
                    if s == 14 and first:
                        split_ffn(1, w2_hi[:, :, :, :].rearrange("p e k d -> p (e k d)"),
                                  w2_lo[:, :, :, :].rearrange("p e k d -> p (e k d)"))

            LOW_AT = (8, 9, 10, 11)
            bodies(pool, body)
            for s in range(STEPS - LAG, STEPS):
                if s == STEPS - LAG + 2:
                    post_rstd(2 * LAST)
                    post_final(LAST, 0)
                normalise(LAST, s)
            post_rstd(2 * NB - 1)
            post_final(LAST, 1)

            def b_rstd(c):
                pool.wait_ge(b_guess_ready, c + 1)
                newton(var_e2, rstd2, newt2, TH, b_newton_step, c, b_rstd_ready)

            def hid_low(c, u):
                pool.wait_ge(hid_hi_ready, E * c + u + 1)
                pool.tensor_tensor(hid_lo[:, u % 4, :, :], hid[:, u % 4, :, :], hid_hi[:, u % 4, :, :],
                                   ALU.subtract).then_inc(hid_lo_ready, 1)

            def body_b(b, par=None):
                for half in range(2):
                    for u in range(E):
                        hid_low(2 * b + half, u)
                        if u == 0 and not (half == 1 and isinstance(b, int) and b == LAST):
                            b_rstd(2 * b + half + 1)

            b_rstd(0)
            bodies(pool, body_b)

        @block.scalar
        def _(act):
            act.wait_ge(w_turned, 1)
            act.activation(wqkv_hi[:], side_tiles(0)[:, 0:3, :], ACT.Copy, scale=WSCALE).then_inc(w_split, 1)
            act.activation(woT[:], side_tiles(0)[:, 3, :], ACT.Copy).then_inc(w_split, 1)
            act.wait_ge(w_turned, 2)
            act.activation(vec[:], side(1)[:, 0:E * KH + 3], ACT.Copy).then_inc(w_split, 1)
            act.activation(bq_scaled[:], side(1)[:, E * KH:E * KH + 1], ACT.Copy, scale=QSCALE).then_inc(w_split, 1)
            act.activation(bv_total[:], side(1)[:, E * KH + 2:E * KH + 3], ACT.Copy, scale=float(T)).then_inc(w_split, 1)

            def prep_xn(bb, c):
                act.wait_ge(shift_ready, bb + 1)
                wait(act, xn_bo_ready, bb)
                for t in range(c * TH, c * TH + TH):
                    ins = act.activation(xn[:, t, :], x1_tiles(bb)[:, t, :], ACT.Identity,
                                         bias=shift[:, t:t + 1], scale=rstd[:, t:t + 1])
                ins.then_inc(xn_ready, 1)

            def post_y(n):
                act.wait_ge(shift2_ready, n + 1)
                for t in range(TH):
                    ins = act.activation(res[:, t, :], res[:, t, :], ACT.Identity,
                                         bias=shift2[:, t:t + 1], scale=rstd2[:, t:t + 1])
                ins.then_inc(y_ready, 1)

            def xT_high(bb, c, bank=0):
                act.wait_ge(xT_done, 2 * bb + c + 1)
                act.activation(xT_hi[:, c, :], side(bank), ACT.Copy).then_inc(xT_hi_ready, 1)

            def qk_bias(bb, i, bank=0):
                act.wait_ge(qk_proj_done, 4 * bb + i + 1)
                act.activation(qk[:, i, :], side(bank), ACT.Identity,
                               bias=bq_scaled[:] if i < 2 else vec[:, E * KH + 1:E * KH + 2],
                               scale=(QSCALE if i < 2 else 1.0) / WSCALE).then_inc(qk_ready, 1)

            def v_copy(bb, par, c, bank=0):
                act.wait_ge(v_proj_done, 2 * bb + c + 1)
                act.activation(v_sb[:, par, c * TH:c * TH + TH, :], side_tiles(bank), ACT.Copy,
                               scale=1.0 / WSCALE).then_inc(v_ready, 1)

            def ctx_copy(b, s):
                g = STEPS * b + s
                act.wait_ge(ctx_done, g + 1)
                wait(act, chunk_added, g - RING + 1)
                act.activation(ctx_sb[:, s % RING, :], sum_ps[:, s % 2, :], ACT.Copy).then_inc(ctx_copied, 1)

            def ctxT_out(n):
                act.wait_ge(chunk_added, T * (n + 1))
                wait(act, wo_done, n)
                act.activation(ctxT[:], ctx_acc[:], ACT.Identity, bias=bv_total[:]).then_inc(ctxT_ready, 1)

            act.wait_ge(w_split, 5)
            for c in range(2):
                prep_xn(0, c)
            for c in range(2):
                xT_high(0, c, c)
            for i in range(4):
                qk_bias(0, i, i % 2)
            for c in range(2):
                v_copy(0, 0, c, c)
            for k in range(T):
                act.wait_ge(mask_turned, k + 1)
                act.activation(limit[:, k, :], side(k % 2).bitcast(BF16), ACT.Copy, bias=-LIMIT).then_inc(limit_ready, 1)

            def exp(b, s):
                for u in range(2):
                    act.wait_ge(clip_done, 2 * STEPS * b + 2 * s + u + 1)
                    wait(act, den_added, STEPS * b + s - 1)
                    act.activation(probs[:, s % 2, 2 * u:2 * u + 2, :], clipped[:, s % 2, 2 * u:2 * u + 2, :],
                                   ACT.Exp).then_inc(exp_done, 1)
                    if u == 0:
                        if s:
                            ctx_copy(b, s - 1)
                        elif not (isinstance(b, int) and b == 0):
                            ctx_copy(b - 1, STEPS - 1)

            def body(b, par=None):
                par = b % 2 if par is None else par
                first, last = isinstance(b, int) and b == 0, isinstance(b, int) and b == LAST
                for s in range(STEPS):
                    exp(b, s)
                    if not last:
                        if s in (2, 3):
                            prep_xn(b + 1, s - 2)
                        if s in (4, 5):
                            xT_high(b + 1, s - 4)
                        if s in (6, 7, 8, 9):
                            qk_bias(b + 1, s - 6)
                        if s in (11, 12):
                            v_copy(b + 1, 1 - par, s - 11)
                    if s == 5 and not first:
                        post_y(2 * b - 2)
                    if s == 14 and not first:
                        post_y(2 * b - 1)
                    if s == 6 and not first:
                        ctxT_out(2 * b - 1)
                    if s == 15:
                        ctxT_out(2 * b)

            bodies(act, body)
            ctx_copy(LAST, STEPS - 1)
            post_y(2 * LAST)
            ctxT_out(2 * NB - 1)
            post_y(2 * LAST + 1)

            def x2T_high(c, par):
                act.wait_ge(x2T_done, c + 1)
                act.activation(x2T_hi[:, par, :], side(0), ACT.Copy).then_inc(x2T_hi_ready, 1)

            def gate_exps(c):
                act.wait_ge(gate_dve, GATE_OPS * c + 3)
                act.activation(logit[:], logit[:], ACT.Exp).then_inc(gate_exp, 1)

            def gelu(c, u):
                n = E * c + u
                for k in range(KH):
                    act.wait_ge(z_done, 2 * n + k + 1)
                    if k == 0:
                        wait(act, hid_lo_ready, n - 3)
                    act.activation(hid[:, u % 4, k, :], score_ps[:, 2 * (u % 2) + k, :], ACT.Gelu,
                                   bias=vec[:, KH * u + k:KH * u + k + 1], scale=1.0 / WSCALE).then_inc(gelu_done, 1)

            def body_b(b, par=None):
                for half in range(2):
                    c = 2 * b + half
                    final = half == 1 and isinstance(b, int) and b == LAST
                    for u in range(E):
                        gelu(c, u)
                        if u == 2 and not final:
                            x2T_high(c + 1, 1 - half)
                        if u == 4 and not final:
                            gate_exps(c + 1)

            x2T_high(0, 0)
            gate_exps(0)
            bodies(act, body_b)

        @block.vector
        def _(dve):
            def rstd_guess(bb, n, st, mean, sq, var_, y, step, done):
                at = STAT_STEPS * bb
                dve.wait_ge(step, at + 1)
                dve.tensor_tensor(mean[:, 0:n], st[:, 0:n, 1], st[:, 0:n, 4], ALU.add)
                dve.tensor_tensor(var_[:, 0:n], st[:, 0:n, 2], st[:, 0:n, 5], ALU.add)
                dve.tensor_tensor(sq[:, 0:n], st[:, 0:n, 1], st[:, 0:n, 4], ALU.subtract).then_inc(step, 1)
                dve.wait_ge(step, at + 2)
                dve.tensor_tensor(sq[:, 0:n], sq[:, 0:n], sq[:, 0:n], ALU.mult).then_inc(step, 1)
                dve.tensor_scalar(mean[:, 0:n], mean[:, 0:n], -0.5, None, ALU.mult)
                dve.wait_ge(step, at + 3)
                dve.scalar_tensor_tensor(out=var_[:, 0:n], in0=sq[:, 0:n], scalar=D / 4.0, in1=var_[:, 0:n],
                                         op0=ALU.mult, op1=ALU.add).then_inc(step, 1)
                dve.wait_ge(step, at + 4)
                dve.tensor_scalar(var_[:, 0:n], var_[:, 0:n], 0.5 / D, 0.5 * EPS, ALU.mult, ALU.add).then_inc(step, 1)
                dve.wait_ge(step, at + 5)
                dve.tensor_scalar(y[:, 0:n].bitcast(I32), var_[:, 0:n].bitcast(I32), 1, None,
                                  ALU.logical_shift_right).then_inc(step, 1)
                dve.wait_ge(step, at + 6)
                dve.tensor_scalar(y[:, 0:n].bitcast(I32), y[:, 0:n].bitcast(I32), -1.0, RSQRT_MAGIC,
                                  ALU.mult, ALU.add).then_inc(done, 1)

            def prep_stats(bb, c):
                dve.wait_ge(x_loaded, 16 * (bb + 1))
                for t in range(c * TH, c * TH + TH):
                    ins = dve.bn_stats(stats[:, t, :], x1_tiles(bb)[:, t, :])
                if c:
                    ins.then_inc(norm_step, 1)

            def prep_guess(bb):
                rstd_guess(bb, T, stats, mean, msq, var_e, rstd, norm_step, guess_ready)

            def xT_low(bb, c, bank=0):
                dve.wait_ge(xT_hi_ready, 2 * bb + c + 1)
                dve.tensor_tensor(xT_lo[:, c, :], side(bank), xT_hi[:, c, :], ALU.subtract).then_inc(xT_lo_ready, 1)

            def qk_high(bb, i):
                dve.wait_ge(qk_ready, 4 * bb + i + 1)
                dve.tensor_copy(qk_hi[:, i, :], qk[:, i, :]).then_inc(qk_hi_ready, 1)

            def clip(b, s):
                for u in range(2):
                    dve.wait_ge(qk_done, 2 * STEPS * b + 2 * s + u + 1)
                    wait(dve, exp_done, 2 * STEPS * b + 2 * s + u - 3)
                    k, half = s % T, s // T
                    dve.scalar_tensor_tensor(
                        out=clipped[:, s % 2, 2 * u:2 * u + 2, :], in0=score_ps[:, 2 * u:2 * u + 2, :], scalar=-LIMIT,
                        in1=limit[:, k:k + 1, half * HALF:half * HALF + HALF].to_broadcast([P, 2, HALF]),
                        op0=ALU.max, op1=ALU.min).then_inc(clip_done, 1)

            def invert(b, i):
                G = GROUPS * b + i
                dve.wait_ge(den_added, GROUP * (G + 1))
                wait(dve, rinv_stored, 16 * G)
                dve.reciprocal(rinv[:], den_ps).then_inc(rinv_ready, 1)

            def post_res(b, par, half):
                n = 2 * b + half
                dve.wait_ge(wo_done, n + 1)
                dve.wait_ge(x1_ready, n + 1)
                dve.wait_ge(xn_bo_ready, b + 1)
                dve.tensor_tensor(res[:], side_tiles(0), xn_bo[:, par, half * TH:half * TH + TH, :],
                                  ALU.add).then_inc(res_ready, 1)

            def post_stats(n):
                dve.wait_ge(res_ready, n + 1)
                for t in range(TH):
                    ins = dve.bn_stats(stats2[:, t, :], res[:, t, :])
                ins.then_inc(norm2_step, 1)
                rstd_guess(n, TH, stats2, mean2, msq2, var_e2, rstd2, norm2_step, guess2_ready)

            prep_stats(0, 0)
            prep_stats(0, 1)
            prep_guess(0)
            dve.wait_ge(w_split, 2)
            dve.scalar_tensor_tensor(out=wqkv_lo[:], in0=side_tiles(0)[:, 0:3, :], scalar=WSCALE, in1=wqkv_hi[:],
                                     op0=ALU.mult, op1=ALU.subtract).then_inc(w_low, 1)
            for c in range(2):
                xT_low(0, c, c)
            for i in range(4):
                qk_high(0, i)
            for t in range(T):
                dve.wait_ge(adj_loaded[t], 16)
                dve.tensor_scalar(mask20[:, t, :, :], adj_raw[t].rearrange("p (k q) -> p k q", k=T), 0.0, 2 * LIMIT,
                                  ALU.not_equal, ALU.mult).then_inc(mask_made, 1)

            def body(b, par=None):
                par = b % 2 if par is None else par
                first, last = isinstance(b, int) and b == 0, isinstance(b, int) and b == LAST
                for s in range(STEPS):
                    if first and s < T:
                        dve.wait_ge(limit_ready, s + 1)
                    if first and s == 0:
                        dve.wait_ge(mask_turned, T)
                    clip(b, s)
                    if s % GROUP == 0:
                        if s:
                            invert(b, s // GROUP - 1)
                        elif not first:
                            invert(b - 1, GROUPS - 1)
                    if not last:
                        if s in (0, 1):
                            prep_stats(b + 1, s)
                        if s == 1:
                            prep_guess(b + 1)
                        if s in (5, 6):
                            xT_low(b + 1, s - 5)
                        if s in (7, 8, 9, 10):
                            qk_high(b + 1, s - 7)
                    if not first:
                        if s == 2:
                            post_res(b - 1, 1 - par, 0)
                        if s == 3:
                            post_stats(2 * b - 2)
                        if s == 11:
                            post_res(b - 1, 1 - par, 1)
                            post_stats(2 * b - 1)

            bodies(dve, body)
            invert(LAST, GROUPS - 1)
            post_res(LAST, LAST % 2, 0)
            post_stats(2 * LAST)
            post_res(LAST, LAST % 2, 1)
            post_stats(2 * LAST + 1)

            def x1_half(b, half):
                return x1[:, b, half * HALF:half * HALF + HALF].rearrange("p (t d) -> p t d", t=TH)

            def b_stats(b, half):
                c = 2 * b + half
                for t in range(TH):
                    ins = dve.bn_stats(stats2[:, t, :], x1[:, b, (half * TH + t) * P:(half * TH + t + 1) * P])
                ins.then_inc(b_norm_step, 1)
                rstd_guess(c, TH, stats2, mean2, msq2, var_e2, rstd2, b_norm_step, b_guess_ready)

            def b_xn(b, half):
                c = 2 * b + half
                dve.wait_ge(b_rstd_ready, c + 1)
                for t in range(TH):
                    ins = dve.tensor_scalar(xn2[:, t, :], x1[:, b, (half * TH + t) * P:(half * TH + t + 1) * P],
                                            mean2[:, t:t + 1], rstd2[:, t:t + 1], ALU.add, ALU.mult)
                ins.then_inc(xn2_ready, 1)

            def b_low(c, par):
                dve.wait_ge(x2T_hi_ready, c + 1)
                dve.tensor_tensor(x2T_lo[:, par, :], side(0), x2T_hi[:, par, :], ALU.subtract).then_inc(x2T_lo_ready, 1)

            def b_logits(c):
                at = GATE_OPS * c
                dve.wait_ge(gate_done, c + 1)
                dve.scalar_tensor_tensor(out=logit[:], in0=side(1)[:, 0:TH * E].rearrange("p (t e) -> p t e", t=TH),
                                         scalar=1.0 / WSCALE,
                                         in1=gate_b_bc[:, :].rearrange("p (o e) -> p o e", o=1).to_broadcast([P, TH, E]),
                                         op0=ALU.mult, op1=ALU.add).then_inc(gate_dve, 1)
                dve.wait_ge(gate_dve, at + 1)
                dve.tensor_reduce(gsum[:], logit[:], AX.X, ALU.max).then_inc(gate_dve, 1)
                dve.wait_ge(gate_dve, at + 2)
                dve.tensor_tensor(logit[:], logit[:], gsum[:, :].rearrange("p (t o) -> p t o", o=1).to_broadcast([P, TH, E]),
                                  ALU.subtract).then_inc(gate_dve, 1)

            def b_weights(c):
                at = GATE_OPS * c
                dve.wait_ge(gate_exp, c + 1)
                dve.tensor_reduce(gsum[:], logit[:], AX.X, ALU.add).then_inc(gate_dve, 1)
                dve.wait_ge(gate_dve, at + 4)
                dve.reciprocal(gsum[:], gsum[:]).then_inc(gate_dve, 1)
                dve.wait_ge(gate_dve, at + 5)
                dve.tensor_tensor(gprob[:], logit[:], gsum[:, :].rearrange("p (t o) -> p t o", o=1).to_broadcast([P, TH, E]),
                                  ALU.mult).then_inc(gate_dve, 1)
                dve.wait_ge(gate_dve, at + 6)
                dve.tensor_scalar(gprob_s[:], gprob[:], 1.0 / WSCALE, None, ALU.mult)
                for t in range(TH):
                    ins = dve.max(top[:, t, :], gprob[:, t, :])
                ins.then_inc(gate_dve, 1)

            def b_top_known(c):
                dve.wait_ge(gate_dve, GATE_OPS * c + 7)

            def b_picks(c, par):
                at = GATE_OPS * c
                for t in range(TH):
                    ins = dve.max_index(top_at[:, t, :], top[:, t, :], gprob[:, t, :])
                ins.then_inc(gate_dve, 1)
                dve.wait_ge(gate_dve, at + 8)
                dve.tensor_copy(top_no[:], top_at[:, :, 0:2]).then_inc(gate_dve, 1)
                dve.wait_ge(gate_dve, at + 9)
                for j in range(2):
                    ins = dve.tensor_tensor(
                        pick[:, j, :, :], expert_no[:, :].rearrange("p (o e) -> p o e", o=1).to_broadcast([P, TH, E]),
                        top_no[:, :, j:j + 1].to_broadcast([P, TH, E]), ALU.is_equal)
                ins.then_inc(gate_dve, 1)
                dve.wait_ge(gate_dve, at + 10)
                dve.tensor_tensor(pick[:, 0, :, :], pick[:, 0, :, :], pick[:, 1, :, :], ALU.add).then_inc(gate_dve, 1)
                dve.wait_ge(gate_dve, at + 11)
                dve.tensor_tensor(cw_s[:, par, :, :], pick[:, 0, :, :], gprob_s[:], ALU.mult)
                dve.tensor_tensor(cw[:], pick[:, 0, :, :], gprob[:], ALU.mult).then_inc(cw_ready, 1)

            def b_cwT(c):
                dve.wait_ge(cwT_done, c + 1)
                dve.tensor_copy(cwT, side(1)[0:E, :]).then_inc(cwT_ready, 1)

            def b_start(b, half):
                c = 2 * b + half
                dve.wait_ge(b2_done, c + 1)
                wait(dve, stored[half], 16 * b)
                dve.tensor_tensor(acc[:, half, :, :], side_tiles(0), x1_half(b, half), ALU.add).then_inc(acc_start, 1)

            def hid_high(c, u):
                n = E * c + u
                dve.wait_ge(gelu_done, 2 * n + 2)
                wait(dve, y_done, n - 3)
                dve.tensor_copy(hid_hi[:, u % 4, :, :], hid[:, u % 4, :, :]).then_inc(hid_hi_ready, 1)

            def add_up(c, half, u):
                n = E * c + u
                dve.wait_ge(y_done, n + 1)
                if u == 0:
                    dve.wait_ge(acc_start, c + 1)
                else:
                    dve.wait_ge(acc_done, n)
                for t in range(TH):
                    ins = dve.scalar_tensor_tensor(out=acc[:, half, t, :], in0=sum_ps[:, u % 2, t * P:t * P + P],
                                                   scalar=cw_s[:, half, t, u:u + 1], in1=acc[:, half, t, :],
                                                   op0=ALU.mult, op1=ALU.add)
                ins.then_inc(acc_done, 1)

            def body_b(b, par=None):
                for half in range(2):
                    c = 2 * b + half
                    nb, nh = (b, 1) if half == 0 else (b + 1, 0)
                    final = half == 1 and isinstance(b, int) and b == LAST
                    for u in range(E):
                        if u == 6 and not final:
                            b_top_known(c + 1)
                        hid_high(c, u)
                        if not (u == 0 and half == 0 and isinstance(b, int) and b == 0):
                            pc, ph, pu = (c, half, u - 1) if u else (c - 1, 1 - half, E - 1)
                            add_up(pc, ph, pu)
                            if u == 0:
                                b_start(b, half)
                        if final:
                            continue
                        if u == 0:
                            b_stats(nb, nh)
                        if u == 1:
                            b_xn(nb, nh)
                        if u == 3:
                            b_low(c + 1, 1 - half)
                        if u == 4:
                            b_logits(c + 1)
                        if u == 5:
                            b_weights(c + 1)
                        if u == 6:
                            b_picks(c + 1, 1 - half)
                        if u == 7:
                            b_cwT(c + 1)

            dve.wait_ge(x1_ready, 2 * NB + 1)
            dve.wait_ge(exp_done, 2 * STEPS * NB)
            dve.wait_ge(den_added, STEPS * NB)
            b_stats(0, 0)
            b_xn(0, 0)
            b_low(0, 0)
            b_logits(0)
            b_weights(0)
            b_top_known(0)
            b_picks(0, 0)
            b_cwT(0)
            b_start(0, 0)
            bodies(dve, body_b)
            add_up(CHUNKS - 1, 1, E - 1)

        @block.tensor
        def _(pe):
            def turn(dst, src, idn):
                return pe.transpose(dst, src, idn)

            def three(dst, a_hi, a_lo, b_hi, b_lo):
                pe.matmul(dst, a_hi, b_hi, start=True, stop=False)
                pe.matmul(dst, a_hi, b_lo, start=False, stop=False)
                return pe.matmul(dst, a_lo, b_hi, start=False, stop=True)

            pe.wait_ge(consts_ready, CONSTS)
            pe.wait_ge(w_loaded, 16 * 8)
            for i in range(4):
                ins = turn(side_tiles(0)[:, i, :], wqkvo_raw[:, i, :], ident[:])
            ins.then_inc(w_turned, 1)
            pe.matmul(side(1)[:, 0:E * KH + 3], vec_raw[:], ident[0:E * KH + 3, 0:E * KH + 3],
                      start=True, stop=True).then_inc(w_turned, 1)

            def xT(bb, c, bank=0):
                pe.wait_ge(xn_ready, 2 * bb + c + 1)
                for t in range(TH):
                    ins = turn(side_tiles(bank)[:, t, :], xn[:, c * TH + t, :], ident[:])
                ins.then_inc(xT_done, 1)

            def qk_proj(bb, i, bank=0):
                c = i % 2
                pe.wait_ge(xT_lo_ready, 2 * bb + c + 1)
                three(side(bank), wqkv_hi[:, i // 2, :], wqkv_lo[:, i // 2, :], xT_hi[:, c, :],
                      xT_lo[:, c, :]).then_inc(qk_proj_done, 1)

            def v_proj(bb, c, bank=0):
                for t in range(TH):
                    ins = three(side_tiles(bank)[:, t, :], xT_hi[:, c, t * P:t * P + P], xT_lo[:, c, t * P:t * P + P],
                                wqkv_hi[:, 2, :], wqkv_lo[:, 2, :])
                ins.then_inc(v_proj_done, 1)

            def scores(b, par, s):
                k, half = s % T, s // T
                if s == 0:
                    pe.wait_ge(stacked, 16 * STACKS * (b + 1))
                for u in range(2):
                    wait(pe, clip_done, 2 * STEPS * b + 2 * s + u - 1)
                    for h in (2 * u, 2 * u + 1):
                        ins = pe.matmul(score_ps[:, h, :], kstack[:, par, h, k * P:k * P + P],
                                        qstack[:, par, h, half * HALF:half * HALF + HALF], start=True, stop=True)
                    ins.then_inc(qk_done, 1)

            def sums(b, par, s):
                k, g, G = s % T, STEPS * b + s, GROUPS * b + s // GROUP
                j = s % GROUP
                if s == 0:
                    pe.wait_ge(v_ready, 2 * b + 2)
                pe.wait_ge(exp_done, 2 * g + 2)
                wait(pe, ctx_copied, g - 1)
                for h in range(HEADS):
                    head = slice(DH * h, DH * h + DH)
                    ins = pe.matmul(sum_ps[head, s % 2, :], v_sb[:, par, k, head], probs[:, s % 2, h, :],
                                    start=True, stop=True, tile_position=(0, DH * h))
                ins.then_inc(ctx_done, 1)
                if j == 0:
                    wait(pe, rinv_ready, G)
                for c in range(2):
                    for h in range(HEADS):
                        ins = pe.matmul(den_ps[DH * h:DH * h + DH, :], gather[:, c, j, :],
                                        probs[:, s % 2, h, c * (HALF // 2):(c + 1) * (HALF // 2)],
                                        start=(j == 0 and c == 0), stop=(j == GROUP - 1 and c == 1),
                                        tile_position=(0, DH * h))
                ins.then_inc(den_added, 1)

            def wo(n):
                pe.wait_ge(ctxT_ready, n + 1)
                for t in range(TH):
                    ins = pe.matmul(side_tiles(0)[:, t, :], ctxT[:, t * P:t * P + P], woT[:], start=True, stop=True)
                ins.then_inc(wo_done, 1)

            pe.wait_ge(w_split, 5)
            pe.wait_ge(w_low, 1)
            for c in range(2):
                xT(0, c, c)
            for i in range(4):
                if i >= 2:
                    pe.wait_ge(qk_ready, i - 1)
                qk_proj(0, i, i % 2)
            for c in range(2):
                pe.wait_ge(qk_ready, 3 + c)
                v_proj(0, c, c)
            pe.wait_ge(mask_made, T)
            for k in range(T):
                if k < 2:
                    pe.wait_ge(v_ready, k + 1)
                else:
                    pe.wait_ge(limit_ready, k - 1)
                for t in range(T):
                    ins = turn(side(k % 2).bitcast(BF16)[:, t * P:t * P + P], mask20[:, t, k, :], identb[:])
                ins.then_inc(mask_turned, 1)
            scores(0, 0, 0)

            def body(b, par=None):
                par = b % 2 if par is None else par
                first, last = isinstance(b, int) and b == 0, isinstance(b, int) and b == LAST
                m, n, bb = 2 * b - 1, 2 * b, b + 1
                for s in range(STEPS):
                    if s + 1 < STEPS:
                        scores(b, par, s + 1)
                    elif not last:
                        scores(b + 1, 1 - par, 0)
                    if s == 0 and first:
                        pe.wait_ge(limit_ready, T)
                    if not last:
                        if s == 4:
                            wait(pe, res_ready, m)
                            xT(bb, 0)
                        if s == 5:
                            pe.wait_ge(xT_lo_ready, 2 * bb + 1)
                            xT(bb, 1)
                        if s in (6, 7, 8, 9):
                            if s == 6:
                                pe.wait_ge(xT_lo_ready, 2 * bb + 2)
                            else:
                                pe.wait_ge(qk_ready, 4 * bb + s - 6)
                            qk_proj(bb, s - 6)
                    if s == 10 and not first:
                        if last:
                            pe.wait_ge(res_ready, m)
                        else:
                            pe.wait_ge(qk_ready, 4 * bb + 4)
                        wo(m)
                    if s == 11 and not last:
                        if first:
                            pe.wait_ge(qk_ready, 4 * bb + 4)
                        else:
                            pe.wait_ge(res_ready, m + 1)
                        v_proj(bb, 0)
                    if s == 12 and not last:
                        pe.wait_ge(v_ready, 2 * bb + 1)
                        v_proj(bb, 1)
                    if s == 1 and not first:
                        pe.wait_ge(v_ready, 2 * b + 2)
                        wo(n - 2)
                    sums(b, par, s)

            bodies(pe, body)
            for n in (2 * LAST, 2 * LAST + 1):
                pe.wait_ge(res_ready, n)
                wo(n)

            def x2T(c):
                pe.wait_ge(xn2_ready, c + 1)
                wait(pe, acc_start, c)
                for t in range(TH):
                    ins = turn(side_tiles(0)[:, t, :], xn2[:, t, :], ident[:])
                ins.then_inc(x2T_done, 1)

            def gate(c, par):
                pe.wait_ge(x2T_lo_ready, c + 1)
                wait(pe, cwT_ready, c)
                for t in range(TH):
                    ins = three(side(1)[:, t * E:t * E + E], x2T_hi[:, par, t * P:t * P + P],
                                x2T_lo[:, par, t * P:t * P + P], gate_hi[:], gate_lo[:])
                ins.then_inc(gate_done, 1)

            def turn_cw(c):
                pe.wait_ge(cw_ready, c + 1)
                for t in range(TH):
                    ins = pe.matmul(side(1)[0:E, t * P:t * P + P], cw[:, t, :], ident[:], start=True, stop=True)
                ins.then_inc(cwT_done, 1)

            def weighted_b2(c):
                pe.wait_ge(cwT_ready, c + 1)
                for t in range(TH):
                    ins = pe.matmul(side_tiles(0)[:, t, :], cwT[:, t * P:t * P + P], b2_sb[:], start=True, stop=True)
                ins.then_inc(b2_done, 1)

            def hidden(c, par, u):
                n = E * c + u
                if u == 0:
                    pe.wait_ge(x2T_lo_ready, c + 1)
                wait(pe, gelu_done, 2 * n - 2)
                for k in range(KH):
                    three(score_ps[:, 2 * (u % 2) + k, :], w1_hi[:, u, k * P:k * P + P], w1_lo[:, u, k * P:k * P + P],
                          x2T_hi[:, par, :], x2T_lo[:, par, :]).then_inc(z_done, 1)

            def second(c, u):
                n = E * c + u
                pe.wait_ge(hid_lo_ready, n + 1)
                wait(pe, acc_done, n - 1)
                for t in range(TH):
                    for k in range(KH):
                        cols = slice(t * P, t * P + P)
                        hi, lo = hid_hi[:, u % 4, k, cols], hid_lo[:, u % 4, k, cols]
                        dst = sum_ps[:, u % 2, cols]
                        pe.matmul(dst, hi, w2_hi[:, u, k, :], start=(k == 0), stop=False)
                        pe.matmul(dst, hi, w2_lo[:, u, k, :], start=False, stop=False)
                        ins = pe.matmul(dst, lo, w2_hi[:, u, k, :], start=False, stop=(k == KH - 1))
                ins.then_inc(y_done, 1)

            pe.wait_ge(res_ready, 2 * NB)
            pe.wait_ge(gate_step, 3)
            pe.wait_ge(ffn_step, 6)
            x2T(0)
            gate(0, 0)
            hidden(0, 0, 0)
            hidden(0, 0, 1)
            turn_cw(0)
            weighted_b2(0)

            def body_b(b, par=None):
                for half in range(2):
                    c = 2 * b + half
                    final = half == 1 and isinstance(b, int) and b == LAST
                    for u in range(E):
                        if u + 2 < E:
                            hidden(c, half, u + 2)
                        elif not final:
                            hidden(c + 1, 1 - half, u + 2 - E)
                        if u == 0 and not (half == 0 and isinstance(b, int) and b == 0):
                            weighted_b2(c)
                        if not final:
                            if u == 2:
                                x2T(c + 1)
                            if u == 4:
                                gate(c + 1, 1 - half)
                            if u == 7:
                                turn_cw(c + 1)
                        second(c, u)

            bodies(pe, body_b)


_INS = ["x", "adj", "L0_gnn_Wq", "L0_gnn_bq", "L0_gnn_Wk", "L0_gnn_bk", "L0_gnn_Wv", "L0_gnn_bv", "L0_gnn_Wo",
        "L0_gnn_bo", "L0_gnn_gamma", "L0_gnn_beta", "L0_ffn_gate_w", "L0_ffn_gate_b", "L0_ffn_W1", "L0_ffn_b1",
        "L0_ffn_W2", "L0_ffn_b2"]


def kernel(**inputs):
    import numpy as np
    import concourse.bacc as bacc
    from concourse.bass_utils import run_bass_kernel_spmd

    nc = bacc.Bacc("TRN2", target_bir_lowering=False, num_devices=1)
    arrays, args = {}, []
    for name in _INS:
        a = np.ascontiguousarray(inputs[name])
        arrays[f"in_{name}"] = a
        args.append(nc.dram_tensor(f"in_{name}", a.shape, mybir.dt.from_np(a.dtype), kind="ExternalInput").ap())
    out = nc.dram_tensor("out_x", inputs["x"].shape, F32, kind="ExternalOutput").ap()
    gnn_moe(nc, *args, out)
    r = run_bass_kernel_spmd(nc, [arrays], core_ids=[0])
    return r.results[0]["out_x"]
```

```python
from contextlib import ExitStack

import concourse.bass as bass
from concourse import mybir

ALU = mybir.AluOpType
ACT = mybir.ActivationFunctionType
AX = mybir.AxisListType
F32 = mybir.dt.float32
F16 = mybir.dt.float16
BF16 = mybir.dt.bfloat16
I32 = mybir.dt.int32
U32 = mybir.dt.uint32

P = 128
WSCALE = 256.0
EPS = 1e-5
LIMIT = 10.0
RSQRT_MAGIC = float(0x5F3759DF - 0x400000)
NEWTON = 3
STAT_STEPS = 7 + 3 * NEWTON


def gnn_moe(nc, x, adj, Wq, bq, Wk, bk, Wv, bv, Wo, bo, gamma, beta, gate_w, gate_b, W1, b1, W2, b2, out):
    NB, N, D = x.shape
    T = N // P
    HEADS, DH = 4, 32
    E, _, HID = W1.shape
    KH = HID // P
    HALF = N // 2
    TH = T // 2
    STEPS = 2 * T
    STACKS = 8
    GROUP = 4
    GROUPS = STEPS // GROUP
    RING = 2 * GROUP
    LAG = GROUP + 3
    assert D == P and HEADS * DH == D and N == 1024 and HALF == 512 and KH == 2 and E == 8
    QSCALE = float(DH) ** -0.5

    ctx = ExitStack()
    with ctx:
        def sb(name, shape, dt):
            return ctx.enter_context(nc.sbuf_tensor(name, shape, dt))

        def sem(name):
            return ctx.enter_context(nc.semaphore(name))

        ident = sb("ident", [P, P], F32)
        identb = sb("identb", [P, P], BF16)
        expert_no = sb("expert_no", [P, E], F32)
        vec = sb("vec", [P, E * KH + 3], F32)
        bq_scaled = sb("bq_scaled", [P, 1], F32)
        bv_total = sb("bv_total", [P, 1], F32)
        wqkv_hi = sb("wqkv_hi", [P, 3, P], F16)
        wqkv_lo = sb("wqkv_lo", [P, 3, P], F16)
        woT = sb("woT", [P, P], F32)
        rows_bc = sb("rows_bc", [P, 3, P], F32)
        gate_b_bc = sb("gate_b_bc", [P, E], F32)
        gate_raw = sb("gate_raw", [P, E], F32)
        gate_hi = sb("gate_hi", [P, E], F16)
        gate_lo = sb("gate_lo", [P, E], F16)
        w1_hi = sb("w1_hi", [P, E, HID], F16)
        w1_lo = sb("w1_lo", [P, E, HID], F16)
        w2_hi = sb("w2_hi", [P, E, KH, P], F16)
        w2_lo = sb("w2_lo", [P, E, KH, P], F16)
        b2_sb = sb("b2_sb", [E, P], F32)
        limit = sb("limit", [P, T, N], BF16)
        x1 = sb("x1", [P, NB, T * P], F32)
        ctx_sb = sb("ctx_sb", [P, RING, HALF], F32)
        adj_raw = [x1[:, NB - 4 + t, :].bitcast(I32) for t in range(4)] + \
            [ctx_sb[:, 2 * t:2 * t + 2, :].rearrange("p r n -> p (r n)").bitcast(I32) for t in range(T - 4)]
        w_raw = [x1[:, NB - 4 + 2 * i:NB - 2 + 2 * i, :].rearrange("p b n -> p (b n)") for i in range(2)]
        xn = sb("xn", [P, T, P], F32)
        xn_bo = sb("xn_bo", [P, 2, T, P], F32)
        xT_hi = sb("xT_hi", [P, 2, HALF], F16)
        xT_lo = sb("xT_lo", [P, 2, HALF], F16)
        qk = sb("qk", [P, 4, HALF], F32)
        qk_hi = sb("qk_hi", [P, 4, HALF], F16)
        qk_lo = sb("qk_lo", [P, 4, HALF], F16)
        qstack = sb("qstack", [P, 2, HEADS, N], F16)
        kstack = sb("kstack", [P, 2, HEADS, N], F16)
        v_sb = sb("v_sb", [P, 2, T, P], F32)
        gather = sb("gather", [P, 2, GROUP, DH], F32)
        clip_buf = sb("clip_buf", [P, 2 * HEADS * HALF], F32)
        prob_buf = sb("prob_buf", [P, 2 * HEADS * HALF], F32)
        clipped = clip_buf[:, :].rearrange("p (r h n) -> p r h n", r=2, h=HEADS)
        probs = prob_buf[:, :].rearrange("p (r h n) -> p r h n", r=2, h=HEADS)
        mask20 = clip_buf[:, :].bitcast(BF16).rearrange("p (t k q) -> p t k q", t=T, k=T)
        rinv = sb("rinv", [P, HALF // 2], F32)
        rspread = sb("rspread", [P, GROUP, HALF], F32)
        ctx_acc = sb("ctx_acc", [P, HALF], F32)
        ctxT = sb("ctxT", [P, HALF], F32)
        vec_raw = ctxT[0:E * KH + 3, 0:P]
        res = sb("res", [P, TH, P], F32)
        wqkvo_raw = res
        stats = sb("stats", [P, 4 * T, 6], F32)
        mean, shift, msq, var_e, rstd = [
            sb(name, [P, NB * T], F32) for name in ("mean", "shift", "msq", "var_e", "rstd")]
        shift2 = sb("shift2", [P, TH], F32)
        stats2 = sb("stats2", [P, TH, 6], F32)
        mean2 = sb("mean2", [P, TH], F32)
        msq2 = sb("msq2", [P, TH], F32)
        var_e2 = sb("var_e2", [P, TH], F32)
        rstd2 = sb("rstd2", [P, TH], F32)
        hid = ctx_sb[:, :, :].rearrange("p (r k) n -> p r k n", k=KH)
        acc = clip_buf[:, 0:2 * HALF].rearrange("p (r t d) -> p r t d", r=2, t=TH)
        hid_hi = prob_buf[:, 0:2 * KH * HALF].bitcast(F16).rearrange("p (r k n) -> p r k n", r=4, k=KH)
        hid_lo = prob_buf[:, 2 * KH * HALF:4 * KH * HALF].bitcast(F16).rearrange("p (r k n) -> p r k n", r=4, k=KH)
        def from_limit(first, *dims):
            size = 1
            for d in dims:
                size *= d
            flat = limit[:, :, :].rearrange("p t n -> p (t n)").bitcast(F32)[:, first:first + size]
            return flat.rearrange("p (a b) -> p a b", b=dims[-1]) if len(dims) == 2 else flat

        TILES = NB * T
        SPANS = (slice(0, TILES - T), slice(TILES - T, TILES))
        mean_b, msq_b, var_b, rstd_b, shift_b = mean, msq, var_e, rstd, shift
        gsum = from_limit(0, TILES)
        stats_b = from_limit(TILES * (3 + 6 * E), TILES, 6)
        logit, top, top_at, gprob, pick0, pick1 = [from_limit(TILES * (1 + E * i), TILES, E) for i in range(6)]
        top_at = top_at.bitcast(U32)
        top_no = from_limit(TILES * (1 + 6 * E), TILES, 2)
        x2T_hi = qstack[:, :, :, :].rearrange("p a h n -> p (a h n)").rearrange("p (c n) -> p c n", n=HALF)
        x2T_lo = kstack[:, :, :, :].rearrange("p a h n -> p (a h n)").rearrange("p (c n) -> p c n", n=HALF)
        cw_all = qk[:, 0, :].rearrange("p (t e) -> p t e", e=E)
        cw_chunks = qk[:, 0, :].rearrange("p (c t e) -> p c t e", t=TH, e=E)
        xn2 = qk[:, 2:4, :].rearrange("p r (t d) -> p r t d", t=TH)
        cw = sb("cw", [P, 2, TH, E], F32)
        cw_s = sb("cw_s", [P, 2, TH, E], F32)
        cwT = rspread[0:E, 0, :]

        score_ps = ctx.enter_context(nc.psum_tensor("score_ps", [P, 4, HALF], F32))
        sum_ps = ctx.enter_context(nc.psum_tensor("sum_ps", [P, 2, HALF], F32))
        side_ps = ctx.enter_context(nc.psum_tensor("side_ps", [P, 2, HALF], F32))
        den_ps = side_ps[:, 1, 0:HALF // 2]
        logits_ps = score_ps[:, 0, :].rearrange("p (c n) -> p c n", n=TH * E)

        qk_dram = nc.dram_tensor("qk_dram", (4, P, N), F16, kind="Internal").ap()
        den_dram = nc.dram_tensor("den_dram", (2, P, HALF // 2), F32, kind="Internal").ap()

        def side(i):
            return side_ps[:, i, :]

        def side_tiles(i):
            return side_ps[:, i, :].rearrange("p (t d) -> p t d", t=TH)

        consts_ready = sem("consts_ready")
        w_loaded = sem("w_loaded")
        rows_loaded = sem("rows_loaded")
        adj_loaded = [sem(f"adj_loaded{t}") for t in range(T)]
        ffn_w_loaded = sem("ffn_w_loaded")
        w_turned = sem("w_turned")
        w_split = sem("w_split")
        w_low = sem("w_low")
        mask_made = sem("mask_made")
        mask_turned = sem("mask_turned")
        limit_ready = sem("limit_ready")
        ffn_step = sem("ffn_step")
        gate_step = sem("gate_step")
        x_loaded = [sem(f"x_loaded{i}") for i in range(3)]
        norm_step = sem("norm_step")
        shift_ready = sem("shift_ready")
        shift2_ready = sem("shift2_ready")
        xn_ready = sem("xn_ready")
        xT_done = sem("xT_done")
        xT_hi_ready = sem("xT_hi_ready")
        xT_lo_ready = sem("xT_lo_ready")
        qk_proj_done = sem("qk_proj_done")
        qk_ready = sem("qk_ready")
        qk_hi_ready = sem("qk_hi_ready")
        qk_lo_ready = sem("qk_lo_ready")
        parts_stored = sem("parts_stored")
        stacked = sem("stacked")
        v_proj_done = sem("v_proj_done")
        v_ready = sem("v_ready")
        x_beta_ready = sem("x_beta_ready")
        xn_bo_ready = sem("xn_bo_ready")
        qk_done = sem("qk_done")
        clip_done = sem("clip_done")
        exp_done = sem("exp_done")
        ctx_done = sem("ctx_done")
        den_added = sem("den_added")
        ctx_copied = sem("ctx_copied")
        rinv_ready = sem("rinv_ready")
        rinv_stored = sem("rinv_stored")
        rspread_loaded = [sem(f"rspread_loaded{j}") for j in range(GROUP)]
        scaled_ready = sem("scaled_ready")
        chunk_added = sem("chunk_added")
        ctxT_ready = sem("ctxT_ready")
        wo_done = sem("wo_done")
        res_ready = sem("res_ready")
        norm2_step = sem("norm2_step")
        y_ready = sem("y_ready")
        y_scaled = sem("y_scaled")
        x1_ready = sem("x1_ready")
        b_norm_step = sem("b_norm_step")
        b_shift_ready = sem("b_shift_ready")
        xn2_even_ready = sem("xn2_even_ready")
        xn2_odd_ready = sem("xn2_odd_ready")
        x2T_done = sem("x2T_done")
        x2T_hi_ready = sem("x2T_hi_ready")
        x2T_lo_ready = sem("x2T_lo_ready")
        gate_done = sem("gate_done")
        gate_dve = sem("gate_dve")
        gate_exp = sem("gate_exp")
        cw_ready = sem("cw_ready")
        cw_copied = sem("cw_copied")
        cwT_done = sem("cwT_done")
        cwT_ready = sem("cwT_ready")
        b2_done = sem("b2_done")
        acc_start = sem("acc_start")
        z_done = sem("z_done")
        gelu_done = sem("gelu_done")
        hid_hi_ready = sem("hid_hi_ready")
        hid_lo_ready = sem("hid_lo_ready")
        y_done = sem("y_done")
        acc_done = sem("acc_done")
        stored = [sem(f"stored{i}") for i in range(2)]
        LAST = NB - 1
        CONSTS = 3 + E + 2 * GROUP + 2
        CHUNKS = 2 * NB
        MIDDLE = NB // 2
        GATE_OPS = 11
        BATCHES = (range(0, 1), range(1, NB - 4), range(NB - 4, NB))

        def wait(eng, s, value):
            if not isinstance(value, int) or value > 0:
                eng.wait_ge(s, value)

        def bodies(eng, body):
            body(0)
            with eng.Fori(0, (NB - 2) // 2) as i:
                body(2 * i + 1, 1)
                body(2 * i + 2, 0)
            body(LAST)

        out_v = out.rearrange("b (c t p) d -> b c p t d", c=2, t=TH)

        def from_all(v, b, t):
            return v.rearrange("p (b t) -> p b t", t=T)[:, b, t:t + 1]

        def x1_tiles(b):
            return x1[:, b, :].rearrange("p (t d) -> p t d", t=T)

        block = ctx.enter_context(nc.Block())

        @block.sync
        def _(sp):
            def load_x(i):
                first, end = BATCHES[i].start, BATCHES[i].stop
                sp.dma_start(x1[:, first:end, :].rearrange("p b (t d) -> p (b t) d", d=D),
                             x[first:end].rearrange("b (t p) d -> p (b t) d", p=P)).then_inc(x_loaded[i], 16)

            load_x(0)
            for i, w in enumerate((Wq, Wk, Wv, Wo)):
                sp.dma_start(wqkvo_raw[:, i, :], w).then_inc(w_loaded, 16)
            sp.dma_start(vec_raw[0:E * KH, :], b1.rearrange("e (k p) -> (e k) p", p=P)).then_inc(w_loaded, 16)
            for i, v in enumerate((bq, bk, bv)):
                sp.dma_start(vec_raw[E * KH + i:E * KH + i + 1, :], v.rearrange("(o d) -> o d", o=1)).then_inc(w_loaded, 16)
            load_x(1)
            adj_v = adj.rearrange("(t p) k -> p t k", t=T)
            for t in range(T):
                sp.dma_start(adj_raw[t], adj_v[:, t, :]).then_inc(adj_loaded[t], 16)
            for i, v in enumerate((bo, gamma, beta)):
                sp.dma_start(rows_bc[:, i, :], v.partition_broadcast(P)).then_inc(rows_loaded, 16)
            sp.dma_start(gate_b_bc[:], gate_b.partition_broadcast(P)).then_inc(rows_loaded, 16)
            sp.dma_start(gate_raw[:], gate_w).then_inc(rows_loaded, 16)
            sp.dma_start(b2_sb[:], b2).then_inc(rows_loaded, 16)
            sp.wait_ge(mask_made, T)
            sp.dma_start(w_raw[0].rearrange("p (e h) -> p e h", e=E),
                         W1.rearrange("e d h -> d e h")).then_inc(ffn_w_loaded, 16)
            sp.dma_start(w_raw[1].rearrange("p (e k d) -> p e k d", e=E, k=KH),
                         W2.rearrange("e (k p) d -> p e k d", p=P)).then_inc(ffn_w_loaded, 16)

            def spread(b, i, steps=range(GROUP)):
                G = GROUPS * b + i
                if steps[0] == 0:
                    sp.wait_ge(rinv_ready, G + 1)
                    wait(sp, chunk_added, GROUP * G - GROUP + 1)
                    sp.dma_start(den_dram[i % 2], rinv[:]).then_inc(rinv_stored, 16)
                    sp.wait_ge(rinv_stored, 16 * G + 16)
                rows = den_dram[i % 2].rearrange("(h c j) q -> c j h q", h=HEADS, c=2)
                for j in steps:
                    if j:
                        wait(sp, chunk_added, GROUP * G - GROUP + j + 1)
                    for c in range(2):
                        sp.dma_start(rspread[:, j, c * (HALF // 2):(c + 1) * (HALF // 2)],
                                     rows[c, j].rearrange("h (o q) -> h o q", o=1).to_broadcast([HEADS, DH, HALF // 2])
                                     ).then_inc(rspread_loaded[j], 16)


            def body(b, par=None):
                par = b % 2 if par is None else par
                first, last = isinstance(b, int) and b == 0, isinstance(b, int) and b == LAST
                if not first:
                    spread(b - 1, GROUPS - 1)
                spread(b, 0)
                if first:
                    sp.wait_ge(ffn_step, 6)
                    load_x(2)
                spread(b, 1)
                spread(b, 2)

            bodies(sp, body)
            spread(LAST, GROUPS - 1)

            def store(b, half):
                sp.wait_ge(acc_done, E * (2 * b + half + 1))
                sp.dma_start(out_v[b, half], acc[:, half, :, :]).then_inc(stored[half], 16)

            with sp.Fori(0, NB) as b:
                store(b, 0)
                store(b, 1)
            sp.wait_ge(stored[0], 16 * NB)
            sp.wait_ge(stored[1], 16 * NB)

        @block.gpsimd
        def _(pool):
            pool.memset(ident[:], 0.0).then_inc(consts_ready, 1)
            pool.memset(identb[:], 0.0).then_inc(consts_ready, 1)
            pool.memset(gather[:], 0.0).then_inc(consts_ready, 1)
            pool.memset(mean2[:], 0.0).then_inc(x1_ready, 1)
            for e in range(E):
                pool.memset(expert_no[:, e:e + 1], float(e)).then_inc(consts_ready, 1)
            pool.wait_ge(consts_ready, 3)
            for c in range(2):
                for j in range(GROUP):
                    pool.memset(gather[:, c, j, (DH // 2) * c + j:(DH // 2) * (c + 1):GROUP], 1.0).then_inc(consts_ready, 1)
            for m in (ident, identb):
                pool.affine_select(out=m[:], in_=m[:], compare_op=ALU.not_equal, fill=1.0, base=0,
                                   pattern=[[-1, P]], channel_multiplier=1).then_inc(consts_ready, 1)

            def prep_low(bb, i):
                pool.wait_ge(qk_hi_ready, 4 * bb + i + 1)
                pool.tensor_tensor(qk_lo[:, i, :], qk[:, i, :], qk_hi[:, i, :], ALU.subtract).then_inc(qk_lo_ready, 1)

            def add_beta(bb):
                pool.wait_ge(xn_ready, 2 * bb + 2)
                pool.tensor_tensor(x1_tiles(bb), x1_tiles(bb), rows_bc[:, 2:3, :].to_broadcast([P, T, P]),
                                   ALU.add).then_inc(x_beta_ready, 1)

            def prep_xn_bo(bb, par):
                wait(pool, res_ready, 2 * (bb - 1))
                pool.tensor_tensor(xn_bo[:, par, :, :], xn[:], rows_bc[:, 0:1, :].to_broadcast([P, T, P]),
                                   ALU.add).then_inc(xn_bo_ready, 1)

            def normalise(b, s):
                g, k, half = STEPS * b + s, s % T, s // T
                n = 2 * b + half
                pool.wait_ge(ctx_copied, g + 1)
                pool.wait_ge(rspread_loaded[s % GROUP], 32 * (GROUPS * b + s // GROUP + 1))
                fresh, by = ctx_sb[:, s % RING, :], rspread[:, s % GROUP, :]
                if k == 0:
                    wait(pool, ctxT_ready, n)
                    pool.tensor_tensor(ctx_acc[:], fresh, by, ALU.mult).then_inc(chunk_added, 1)
                else:
                    pool.wait_ge(chunk_added, g)
                    pool.tensor_tensor(fresh, fresh, by, ALU.mult).then_inc(scaled_ready, 1)
                    pool.wait_ge(scaled_ready, (T - 1) * n + k)
                    pool.tensor_tensor(ctx_acc[:], ctx_acc[:], fresh, ALU.add).then_inc(chunk_added, 1)

            def post_final(b, half):
                n = 2 * b + half
                pool.wait_ge(x_beta_ready, b + 1)
                pool.wait_ge(y_ready, n + 1)
                pool.tensor_tensor(res[:], res[:], rows_bc[:, 1:2, :].to_broadcast([P, TH, P]),
                                   ALU.mult).then_inc(y_scaled, 1)
                pool.wait_ge(y_scaled, n + 1)
                x1_half = x1[:, b, half * HALF:half * HALF + HALF].rearrange("p (t d) -> p t d", t=TH)
                pool.tensor_tensor(x1_half, res[:], x1_half, ALU.add).then_inc(x1_ready, 1)

            for i in range(4):
                prep_low(0, i)
            pool.wait_ge(rows_loaded, 16 * 6)
            add_beta(0)
            prep_xn_bo(0, 0)
            pool.tensor_scalar(gate_raw[:], gate_raw[:], WSCALE, 1.0, ALU.mult, ALU.mult).then_inc(gate_step, 1)
            pool.wait_ge(gate_step, 1)
            pool.tensor_scalar(gate_hi[:], gate_raw[:], 1.0, 1.0, ALU.mult, ALU.mult).then_inc(gate_step, 1)
            pool.wait_ge(gate_step, 2)
            pool.tensor_tensor(gate_lo[:], gate_raw[:], gate_hi[:], ALU.subtract).then_inc(gate_step, 1)

            def split_ffn(n, hi, lo):
                pool.wait_ge(ffn_w_loaded, 16 * 2)
                pool.tensor_scalar(w_raw[n], w_raw[n], WSCALE, 1.0, ALU.mult, ALU.mult).then_inc(ffn_step, 1)
                pool.wait_ge(ffn_step, 3 * n + 1)
                pool.tensor_scalar(hi, w_raw[n], 1.0, 1.0, ALU.mult, ALU.mult).then_inc(ffn_step, 1)
                pool.wait_ge(ffn_step, 3 * n + 2)
                pool.tensor_tensor(lo, w_raw[n], hi, ALU.subtract).then_inc(ffn_step, 1)

            def body(b, par=None):
                par = b % 2 if par is None else par
                first, last = isinstance(b, int) and b == 0, isinstance(b, int) and b == LAST
                for s in range(STEPS):
                    if s in LOW_AT and not last:
                        prep_low(b + 1, LOW_AT.index(s))
                    if s == 9 and not first:
                        post_final(b - 1, 0)
                    if s >= LAG:
                        normalise(b, s - LAG)
                    elif not first:
                        normalise(b - 1, s - LAG + STEPS)
                    if s == 15 and not first:
                        post_final(b - 1, 1)
                    if s == 6 and not last:
                        add_beta(b + 1)
                    if s == 14 and not last:
                        prep_xn_bo(b + 1, 1 - par)
                    if s == 0 and first:
                        split_ffn(0, w1_hi[:, :, :].rearrange("p e h -> p (e h)"),
                                  w1_lo[:, :, :].rearrange("p e h -> p (e h)"))
                    if s == 4 and first:
                        split_ffn(1, w2_hi[:, :, :, :].rearrange("p e k d -> p (e k d)"),
                                  w2_lo[:, :, :, :].rearrange("p e k d -> p (e k d)"))

            LOW_AT = (7, 8, 9, 10)
            bodies(pool, body)
            for s in range(STEPS - LAG, STEPS):
                if s == STEPS - LAG + 2:
                    post_final(LAST, 0)
                normalise(LAST, s)
            post_final(LAST, 1)

            def hid_low(c, u):
                for k in range(KH):
                    pool.wait_ge(hid_hi_ready, 2 * (E * c + u) + k + 1)
                    pool.tensor_tensor(hid_lo[:, u % 4, k, :], hid[:, u % 4, k, :], hid_hi[:, u % 4, k, :],
                                       ALU.subtract).then_inc(hid_lo_ready, 1)

            def body_b(b, par=None):
                for half in range(2):
                    for u in range(E):
                        hid_low(2 * b + half, u)

            bodies(pool, body_b)

        @block.scalar
        def _(act):
            act.wait_ge(w_turned, 1)
            act.activation(wqkv_hi[:], side_tiles(0)[:, 0:3, :], ACT.Copy, scale=WSCALE).then_inc(w_split, 1)
            act.activation(woT[:], side_tiles(0)[:, 3, :], ACT.Copy).then_inc(w_split, 1)
            act.wait_ge(w_turned, 2)
            act.activation(vec[:], side(1)[:, 0:E * KH + 3], ACT.Copy).then_inc(w_split, 1)
            act.activation(bq_scaled[:], side(1)[:, E * KH:E * KH + 1], ACT.Copy, scale=QSCALE).then_inc(w_split, 1)
            act.activation(bv_total[:], side(1)[:, E * KH + 2:E * KH + 3], ACT.Copy, scale=float(T)).then_inc(w_split, 1)

            def prep_xn(bb, c):
                if isinstance(bb, int) and bb < 2:
                    act.wait_ge(shift_ready, bb + 1)
                else:
                    act.wait_ge(shift_ready, 3)
                wait(act, xn_bo_ready, bb)
                for t in range(c * TH, c * TH + TH):
                    ins = act.activation(xn[:, t, :], x1_tiles(bb)[:, t, :], ACT.Identity,
                                         bias=from_all(shift[:, :], bb, t), scale=from_all(rstd[:, :], bb, t))
                ins.then_inc(xn_ready, 1)

            def post_y(n):
                act.wait_ge(shift2_ready, n + 1)
                for t in range(TH):
                    ins = act.activation(res[:, t, :], res[:, t, :], ACT.Identity,
                                         bias=shift2[:, t:t + 1], scale=rstd2[:, t:t + 1])
                ins.then_inc(y_ready, 1)

            def xT_high(bb, c, bank=0):
                act.wait_ge(xT_done, 2 * bb + c + 1)
                act.activation(xT_hi[:, c, :], side(bank), ACT.Copy).then_inc(xT_hi_ready, 1)

            def qk_bias(bb, i, bank=0):
                act.wait_ge(qk_proj_done, 4 * bb + i + 1)
                act.activation(qk[:, i, :], side(bank), ACT.Identity,
                               bias=bq_scaled[:] if i < 2 else vec[:, E * KH + 1:E * KH + 2],
                               scale=(QSCALE if i < 2 else 1.0) / WSCALE).then_inc(qk_ready, 1)

            def store_parts(bb, i):
                for part, (ready, src) in enumerate(((qk_hi_ready, qk_hi), (qk_lo_ready, qk_lo))):
                    act.wait_ge(ready, 4 * bb + 2 * i + 2)
                    act.dma_start(qk_dram[2 * i + part].rearrange("p (c n) -> p c n", c=2),
                                  src[:, 2 * i:2 * i + 2, :]).then_inc(parts_stored, 16)

            def stack_parts(bb, par, i):
                both = isinstance(bb, int) and bb == 0
                act.wait_ge(parts_stored, 64 * bb + (64 if both else 32 * i + 32))
                dst, order = ((qstack, (0, 0, 1, 1)), (kstack, (0, 1, 0, 1)))[i]
                for r, part in enumerate(order):
                    if r == 0:
                        wait(act, qk_done, 2 * STEPS * (bb - 1))
                    act.dma_start(dst[DH * r:DH * r + DH, par, :, :],
                                  qk_dram[2 * i + part].rearrange("(h d) n -> d h n", h=HEADS)).then_inc(stacked, 16)

            def v_copy(bb, par, c, bank=0):
                act.wait_ge(v_proj_done, 2 * bb + c + 1)
                act.activation(v_sb[:, par, c * TH:c * TH + TH, :], side_tiles(bank), ACT.Copy,
                               scale=1.0 / WSCALE).then_inc(v_ready, 1)

            def ctx_copy(b, s):
                g = STEPS * b + s
                act.wait_ge(ctx_done, g + 1)
                wait(act, chunk_added, g - RING + 1)
                act.activation(ctx_sb[:, s % RING, :], sum_ps[:, s % 2, :], ACT.Copy).then_inc(ctx_copied, 1)

            def ctxT_out(n):
                act.wait_ge(chunk_added, T * (n + 1))
                wait(act, wo_done, n)
                act.activation(ctxT[:], ctx_acc[:], ACT.Identity, bias=bv_total[:]).then_inc(ctxT_ready, 1)

            act.wait_ge(w_split, 5)
            for c in range(2):
                prep_xn(0, c)
            for c in range(2):
                xT_high(0, c, c)
            for i in range(4):
                qk_bias(0, i, i % 2)
            for c in range(2):
                v_copy(0, 0, c, c)
            for i in range(2):
                store_parts(0, i)
            for k in range(T):
                if k == 3:
                    for i in range(2):
                        stack_parts(0, 0, i)
                act.wait_ge(mask_turned, k + 1)
                act.activation(limit[:, k, :], side(k % 2).bitcast(BF16), ACT.Copy, bias=-LIMIT).then_inc(limit_ready, 1)

            def exp(b, s):
                for u in range(2):
                    act.wait_ge(clip_done, 2 * STEPS * b + 2 * s + u + 1)
                    wait(act, ctx_done, STEPS * b + s - 1)
                    wait(act, den_added, STEPS * b + s - 1)
                    act.activation(probs[:, s % 2, 2 * u:2 * u + 2, :], clipped[:, s % 2, 2 * u:2 * u + 2, :],
                                   ACT.Exp).then_inc(exp_done, 1)
                    if u == 0:
                        if s:
                            ctx_copy(b, s - 1)
                        elif not (isinstance(b, int) and b == 0):
                            ctx_copy(b - 1, STEPS - 1)

            def body(b, par=None):
                par = b % 2 if par is None else par
                first, last = isinstance(b, int) and b == 0, isinstance(b, int) and b == LAST
                for s in range(STEPS):
                    exp(b, s)
                    if not last:
                        if s in (1, 2):
                            prep_xn(b + 1, s - 1)
                        if s in (3, 4):
                            xT_high(b + 1, s - 3)
                        if s in (5, 6, 7, 8):
                            qk_bias(b + 1, s - 5)
                        if s in (12, 13):
                            v_copy(b + 1, 1 - par, s - 12)
                        if s in (8, 11):
                            store_parts(b + 1, s // 11)
                        if s in (10, 12):
                            stack_parts(b + 1, 1 - par, s // 12)
                    if s == 7 and not first:
                        post_y(2 * b - 2)
                    if s == 15 and not first:
                        post_y(2 * b - 1)
                    if s == 7 and not first:
                        ctxT_out(2 * b - 1)
                    if s == 15:
                        ctxT_out(2 * b)

            bodies(act, body)
            ctx_copy(LAST, STEPS - 1)
            post_y(2 * LAST)

            def xn2_even(b):
                wait(act, x2T_done, 2 * b - 1)
                for t in range(TH):
                    ins = act.activation(xn2[:, 0, t, :], x1_tiles(b)[:, t, :], ACT.Identity,
                                         bias=from_all(shift_b, b, t), scale=from_all(rstd_b, b, t))
                ins.then_inc(xn2_even_ready, 1)

            def x2T_high(b, half):
                c = 2 * b + half
                act.wait_ge(x2T_done, c + 1)
                act.activation(x2T_hi[:, c, :], sum_ps[:, half, :], ACT.Copy).then_inc(x2T_hi_ready, 1)

            def gate_weights(c, half):
                wait(act, acc_done, E * (c - 1))
                act.activation(cw[:, half, :, :], cw_chunks[:, c, :, :], ACT.Copy)
                act.activation(cw_s[:, half, :, :], cw_chunks[:, c, :, :], ACT.Copy,
                               scale=1.0 / WSCALE).then_inc(cw_copied, 1)

            def cwT_copy(c):
                act.wait_ge(cwT_done, c + 1)
                wait(act, b2_done, c)
                act.activation(cwT, side(1)[0:E, :], ACT.Copy).then_inc(cwT_ready, 1)

            def gelu(c, u):
                n = E * c + u
                for k in range(KH):
                    act.wait_ge(z_done, 2 * n + k + 1)
                    if k == 0:
                        wait(act, hid_lo_ready, 2 * (n - 3))
                    act.activation(hid[:, u % 4, k, :], score_ps[:, 2 * (u % 2) + k, :], ACT.Gelu,
                                   bias=vec[:, KH * u + k:KH * u + k + 1], scale=1.0 / WSCALE).then_inc(gelu_done, 1)

            def body_b(b, par=None):
                for half in range(2):
                    c = 2 * b + half
                    final = half == 1 and isinstance(b, int) and b == LAST
                    for u in range(E):
                        gelu(c, u)
                        if u == 2 and not final:
                            gate_weights(c + 1, 1 - half)
                        if u == 4 and not final:
                            cwT_copy(c + 1)

            def turn_high(b):
                x2T_high(b, 0)
                if not (isinstance(b, int) and b >= LAST - 1):
                    xn2_even(b + 1)
                x2T_high(b, 1)

            def gate_exps(i):
                act.wait_ge(gate_dve, GATE_OPS * i + 3)
                act.activation(logit[:, SPANS[i], :], logit[:, SPANS[i], :], ACT.Exp).then_inc(gate_exp, 1)

            act.wait_ge(b_shift_ready, 1)
            xn2_even(0)
            turn_high(0)
            with act.Fori(1, MIDDLE) as b:
                turn_high(b)
            ctxT_out(2 * LAST + 1)
            with act.Fori(MIDDLE, LAST - 1) as b:
                turn_high(b)
            turn_high(LAST - 1)
            gate_exps(0)
            post_y(2 * LAST + 1)
            act.wait_ge(b_shift_ready, 2)
            xn2_even(LAST)
            turn_high(LAST)
            gate_exps(1)
            act.wait_ge(cw_ready, 2)
            gate_weights(0, 0)
            cwT_copy(0)
            bodies(act, body_b)

        @block.vector
        def _(dve):
            def rsqrt(part, bb, n, st, mean, sq, var_, y, shift, step, done):
                at = STAT_STEPS * bb
                if part == 0:
                    dve.wait_ge(step, at + 1)
                    dve.tensor_tensor(mean[:, 0:n], st[:, 0:n, 1], st[:, 0:n, 4], ALU.add)
                    dve.tensor_tensor(var_[:, 0:n], st[:, 0:n, 2], st[:, 0:n, 5], ALU.add)
                    dve.tensor_tensor(sq[:, 0:n], st[:, 0:n, 1], st[:, 0:n, 4], ALU.subtract).then_inc(step, 1)
                    dve.wait_ge(step, at + 2)
                    dve.tensor_tensor(sq[:, 0:n], sq[:, 0:n], sq[:, 0:n], ALU.mult).then_inc(step, 1)
                    dve.tensor_scalar(mean[:, 0:n], mean[:, 0:n], -0.5, None, ALU.mult)
                if part == 1:
                    dve.wait_ge(step, at + 3)
                    dve.scalar_tensor_tensor(out=var_[:, 0:n], in0=sq[:, 0:n], scalar=D / 4.0, in1=var_[:, 0:n],
                                             op0=ALU.mult, op1=ALU.add).then_inc(step, 1)
                    dve.wait_ge(step, at + 4)
                    dve.tensor_scalar(var_[:, 0:n], var_[:, 0:n], 0.5 / D, 0.5 * EPS, ALU.mult, ALU.add).then_inc(step, 1)
                if part == 2:
                    dve.wait_ge(step, at + 5)
                    dve.tensor_scalar(y[:, 0:n].bitcast(I32), var_[:, 0:n].bitcast(I32), 1, None,
                                      ALU.logical_shift_right).then_inc(step, 1)
                    dve.wait_ge(step, at + 6)
                    dve.tensor_scalar(y[:, 0:n].bitcast(I32), y[:, 0:n].bitcast(I32), -1.0, RSQRT_MAGIC,
                                      ALU.mult, ALU.add).then_inc(step, 1)
                if part >= 3:
                    i = part - 3
                    dve.wait_ge(step, at + 7 + 3 * i)
                    dve.tensor_tensor(sq[:, 0:n], y[:, 0:n], y[:, 0:n], ALU.mult).then_inc(step, 1)
                    dve.wait_ge(step, at + 8 + 3 * i)
                    dve.scalar_tensor_tensor(out=sq[:, 0:n], in0=sq[:, 0:n], scalar=-1.0, in1=var_[:, 0:n],
                                             op0=ALU.mult, op1=ALU.mult).then_inc(step, 1)
                    dve.wait_ge(step, at + 9 + 3 * i)
                    dve.scalar_tensor_tensor(out=y[:, 0:n], in0=sq[:, 0:n], scalar=1.5, in1=y[:, 0:n],
                                             op0=ALU.add, op1=ALU.mult).then_inc(step, 1)
                    if i == NEWTON - 1:
                        dve.wait_ge(step, at + STAT_STEPS)
                        dve.tensor_tensor(shift[:, 0:n], mean[:, 0:n], y[:, 0:n], ALU.mult).then_inc(done, 1)

            def batches_at(i):
                return BATCHES[2].start if i == 2 else 0

            def prep_stats(i, batches):
                dve.wait_ge(x_loaded[i], 16)
                for bb in batches:
                    for t in range(T):
                        ins = dve.bn_stats(stats[:, (bb - batches_at(i)) * T + t, :], x1_tiles(bb)[:, t, :])
                if batches[-1] == BATCHES[i][-1]:
                    ins.then_inc(norm_step, 1)

            def prep_rsqrt(i):
                span = slice(BATCHES[i].start * T, BATCHES[i].stop * T)
                for part in range(6):
                    rsqrt(part, i, span.stop - span.start, stats[:, span.start - batches_at(i) * T:span.stop - batches_at(i) * T, :], mean[:, span], msq[:, span],
                          var_e[:, span], rstd[:, span], shift[:, span], norm_step, shift_ready)

            def xT_low(bb, c, bank=0):
                dve.wait_ge(xT_hi_ready, 2 * bb + c + 1)
                dve.tensor_tensor(xT_lo[:, c, :], side(bank), xT_hi[:, c, :], ALU.subtract).then_inc(xT_lo_ready, 1)

            def qk_high(bb, i):
                dve.wait_ge(qk_ready, 4 * bb + i + 1)
                dve.tensor_copy(qk_hi[:, i, :], qk[:, i, :]).then_inc(qk_hi_ready, 1)

            def clip(b, s, u):
                dve.wait_ge(qk_done, 2 * STEPS * b + 2 * s + u + 1)
                wait(dve, exp_done, 2 * STEPS * b + 2 * s + u - 3)
                k, half = s % T, s // T
                dve.scalar_tensor_tensor(
                    out=clipped[:, s % 2, 2 * u:2 * u + 2, :], in0=score_ps[:, 2 * u:2 * u + 2, :], scalar=-LIMIT,
                    in1=limit[:, k:k + 1, half * HALF:half * HALF + HALF].to_broadcast([P, 2, HALF]),
                    op0=ALU.max, op1=ALU.min).then_inc(clip_done, 1)

            def invert(b, i):
                G = GROUPS * b + i
                dve.wait_ge(den_added, GROUP * (G + 1))
                wait(dve, rinv_stored, 16 * G)
                dve.reciprocal(rinv[:], den_ps).then_inc(rinv_ready, 1)

            def post_res(b, par, half):
                n = 2 * b + half
                dve.wait_ge(wo_done, n + 1)
                dve.wait_ge(x1_ready, n + 1)
                dve.wait_ge(xn_bo_ready, b + 1)
                dve.tensor_tensor(res[:], side_tiles(0), xn_bo[:, par, half * TH:half * TH + TH, :],
                                  ALU.add).then_inc(res_ready, 1)

            def post_stats(n):
                dve.wait_ge(res_ready, n + 1)
                for t in range(TH):
                    ins = dve.bn_stats(stats2[:, t, :], res[:, t, :])
                ins.then_inc(norm2_step, 1)

            def post_rsqrt(n, part):
                rsqrt(part, n, TH, stats2, mean2, msq2, var_e2, rstd2, shift2, norm2_step, shift2_ready)

            prep_stats(0, BATCHES[0])
            prep_rsqrt(0)
            dve.wait_ge(w_split, 2)
            dve.scalar_tensor_tensor(out=wqkv_lo[:], in0=side_tiles(0)[:, 0:3, :], scalar=WSCALE, in1=wqkv_hi[:],
                                     op0=ALU.mult, op1=ALU.subtract).then_inc(w_low, 1)
            for c in range(2):
                xT_low(0, c, c)
            for i in range(4):
                qk_high(0, i)
            for t in range(T):
                dve.wait_ge(adj_loaded[t], 16)
                dve.tensor_scalar(mask20[:, t, :, :], adj_raw[t].rearrange("p (k q) -> p k q", k=T), 0.0, 2 * LIMIT,
                                  ALU.not_equal, ALU.mult).then_inc(mask_made, 1)
            prep_stats(1, BATCHES[1])
            prep_rsqrt(1)

            def body(b, par=None):
                par = b % 2 if par is None else par
                first, last = isinstance(b, int) and b == 0, isinstance(b, int) and b == LAST
                for s in range(STEPS):
                    if first and s < T:
                        dve.wait_ge(limit_ready, s + 1)
                    if first and s == 0:
                        dve.wait_ge(mask_turned, T)
                    clip(b, s, 0)
                    if not first:
                        if s in (4, 5):
                            post_rsqrt(2 * b - 2, 1 + 2 * (s - 4))
                        if s == 6:
                            post_rsqrt(2 * b - 2, 5)
                        if s == 13:
                            post_stats(2 * b - 1)
                        if s == 14:
                            post_rsqrt(2 * b - 1, 1)
                        if s == 15:
                            post_rsqrt(2 * b - 1, 3)
                            post_rsqrt(2 * b - 1, 4)
                    clip(b, s, 1)
                    if first and s in (9, 10, 11, 13):
                        i = (9, 10, 11, 13).index(s)
                        prep_stats(2, BATCHES[2][i:i + 1])
                    if first and s == 14:
                        prep_rsqrt(2)
                    if not last:
                        if s in (4, 5):
                            xT_low(b + 1, s - 4)
                        if s in (6, 7, 8, 9):
                            qk_high(b + 1, s - 6)
                    if not first:
                        if s == 2:
                            post_res(b - 1, 1 - par, 0)
                        if s == 3:
                            post_stats(2 * b - 2)
                            post_rsqrt(2 * b - 2, 0)
                        if s == 12:
                            post_res(b - 1, 1 - par, 1)
                    if s % GROUP == 0:
                        if s:
                            invert(b, s // GROUP - 1)
                        elif not first:
                            invert(b - 1, GROUPS - 1)
                    if not first:
                        if s in (4, 5):
                            post_rsqrt(2 * b - 2, 2 + 2 * (s - 4))
                        if s == 13:
                            post_rsqrt(2 * b - 1, 0)
                        if s == 14:
                            post_rsqrt(2 * b - 1, 2)
                        if s == 15:
                            post_rsqrt(2 * b - 1, 5)

            bodies(dve, body)
            invert(LAST, GROUPS - 1)
            post_res(LAST, LAST % 2, 0)
            post_stats(2 * LAST)
            for part in range(6):
                post_rsqrt(2 * LAST, part)
            def x1_half(b, half):
                return x1[:, b, half * HALF:half * HALF + HALF].rearrange("p (t d) -> p t d", t=TH)

            def xn2_odd(b):
                wait(dve, x2T_done, 2 * b)
                for t in range(TH):
                    ins = dve.tensor_scalar(xn2[:, 1, t, :], x1_tiles(b)[:, TH + t, :], from_all(mean_b, b, TH + t),
                                            from_all(rstd_b, b, TH + t), ALU.add, ALU.mult)
                ins.then_inc(xn2_odd_ready, 1)

            def x2T_low(b, half):
                c = 2 * b + half
                dve.wait_ge(x2T_hi_ready, c + 1)
                dve.tensor_tensor(x2T_lo[:, c, :], sum_ps[:, half, :], x2T_hi[:, c, :], ALU.subtract).then_inc(x2T_lo_ready, 1)

            def b_stats(i, batches):
                for b in batches:
                    for t in range(T):
                        ins = dve.bn_stats(stats_b[:, b * T + t, :], x1_tiles(b)[:, t, :])
                ins.then_inc(b_norm_step, 1)
                span = SPANS[i]
                for part in range(6):
                    rsqrt(part, i, span.stop - span.start, stats_b[:, span, :], mean_b[:, span], msq_b[:, span],
                          var_b[:, span], rstd_b[:, span], shift_b[:, span], b_norm_step, b_shift_ready)

            def gate(i, chunks):
                span, at = SPANS[i], GATE_OPS * i
                n = span.stop - span.start
                z, prob, biggest, places, numbers = [v[:, span, :] for v in (logit, gprob, top, top_at, top_no)]
                first, second, total = pick0[:, span, :], pick1[:, span, :], gsum[:, span]

                def per_tile(v):
                    return v.rearrange("p (t o) -> p t o", o=1).to_broadcast([P, n, E])

                dve.wait_ge(gate_done, chunks)
                dve.scalar_tensor_tensor(out=z, in0=score_ps[:, 0, :].rearrange("p (t e) -> p t e", e=E)[:, span, :],
                                         scalar=1.0 / WSCALE,
                                         in1=gate_b_bc[:, :].rearrange("p (o e) -> p o e", o=1).to_broadcast([P, n, E]),
                                         op0=ALU.mult, op1=ALU.add).then_inc(gate_dve, 1)
                dve.wait_ge(gate_dve, at + 1)
                dve.tensor_reduce(total, z, AX.X, ALU.max).then_inc(gate_dve, 1)
                dve.wait_ge(gate_dve, at + 2)
                dve.tensor_tensor(z, z, per_tile(total), ALU.subtract).then_inc(gate_dve, 1)
                dve.wait_ge(gate_exp, i + 1)
                dve.tensor_reduce(total, z, AX.X, ALU.add).then_inc(gate_dve, 1)
                dve.wait_ge(gate_dve, at + 4)
                dve.reciprocal(total, total).then_inc(gate_dve, 1)
                dve.wait_ge(gate_dve, at + 5)
                dve.tensor_tensor(prob, z, per_tile(total), ALU.mult).then_inc(gate_dve, 1)
                dve.wait_ge(gate_dve, at + 6)
                for t in range(n):
                    ins = dve.max(biggest[:, t, :], prob[:, t, :])
                ins.then_inc(gate_dve, 1)
                dve.wait_ge(gate_dve, at + 7)
                for t in range(n):
                    ins = dve.max_index(places[:, t, :], biggest[:, t, :], prob[:, t, :])
                ins.then_inc(gate_dve, 1)
                dve.wait_ge(gate_dve, at + 8)
                dve.tensor_copy(numbers, places[:, :, 0:2]).then_inc(gate_dve, 1)
                dve.wait_ge(gate_dve, at + 9)
                for j, pick in enumerate((first, second)):
                    ins = dve.tensor_tensor(
                        pick, expert_no[:, :].rearrange("p (o e) -> p o e", o=1).to_broadcast([P, n, E]),
                        numbers[:, :, j:j + 1].to_broadcast([P, n, E]), ALU.is_equal)
                ins.then_inc(gate_dve, 1)
                dve.wait_ge(gate_dve, at + 10)
                dve.tensor_tensor(first, first, second, ALU.add).then_inc(gate_dve, 1)
                dve.wait_ge(gate_dve, at + 11)
                dve.tensor_tensor(cw_all[:, span, :], first, prob, ALU.mult).then_inc(cw_ready, 1)

            def b_start(b, half):
                c = 2 * b + half
                dve.wait_ge(b2_done, c + 1)
                wait(dve, stored[half], 16 * b)
                dve.tensor_tensor(acc[:, half, :, :], side_tiles(0), x1_half(b, half), ALU.add).then_inc(acc_start, 1)

            def hid_high(c, u):
                n = E * c + u
                wait(dve, y_done, n - 3)
                for k in range(KH):
                    dve.wait_ge(gelu_done, 2 * n + k + 1)
                    dve.tensor_copy(hid_hi[:, u % 4, k, :], hid[:, u % 4, k, :]).then_inc(hid_hi_ready, 1)

            def add_up(c, half, u):
                n = E * c + u
                dve.wait_ge(y_done, n + 1)
                if u == 0:
                    dve.wait_ge(acc_start, c + 1)
                else:
                    dve.wait_ge(acc_done, n)
                for t in range(TH):
                    ins = dve.scalar_tensor_tensor(out=acc[:, half, t, :], in0=sum_ps[:, u % 2, t * P:t * P + P],
                                                   scalar=cw_s[:, half, t, u:u + 1], in1=acc[:, half, t, :],
                                                   op0=ALU.mult, op1=ALU.add)
                ins.then_inc(acc_done, 1)

            def body_b(b, par=None):
                for half in range(2):
                    c = 2 * b + half
                    nb, nh = (b, 1) if half == 0 else (b + 1, 0)
                    final = half == 1 and isinstance(b, int) and b == LAST
                    for u in range(E):
                        hid_high(c, u)
                        if not (u == 0 and half == 0 and isinstance(b, int) and b == 0):
                            pc, ph, pu = (c, half, u - 1) if u else (c - 1, 1 - half, E - 1)
                            add_up(pc, ph, pu)
                        if u == 7 and not final:
                            b_start(nb, nh)

            dve.wait_ge(x1_ready, 2 * LAST + 1)
            dve.wait_ge(exp_done, 2 * STEPS * NB)
            dve.wait_ge(den_added, STEPS * NB)
            dve.wait_ge(ctx_done, STEPS * NB)
            b_stats(0, range(LAST))

            def turn_low(b):
                x2T_low(b, 0)
                if not (isinstance(b, int) and b >= LAST - 1):
                    xn2_odd(b + 1)
                x2T_low(b, 1)

            dve.wait_ge(b_shift_ready, 1)
            xn2_odd(0)
            turn_low(0)
            with dve.Fori(1, MIDDLE) as b:
                turn_low(b)
            post_res(LAST, LAST % 2, 1)
            post_stats(2 * LAST + 1)
            for part in range(6):
                post_rsqrt(2 * LAST + 1, part)
            with dve.Fori(MIDDLE, LAST - 1) as b:
                turn_low(b)
            turn_low(LAST - 1)
            gate(0, 2 * LAST)
            dve.wait_ge(x1_ready, 2 * NB + 1)
            b_stats(1, (LAST,))
            dve.wait_ge(b_shift_ready, 2)
            xn2_odd(LAST)
            turn_low(LAST)
            gate(1, CHUNKS)
            b_start(0, 0)
            bodies(dve, body_b)
            add_up(CHUNKS - 1, 1, E - 1)

        @block.tensor
        def _(pe):
            def turn(dst, src, idn):
                return pe.transpose(dst, src, idn)

            def three(dst, a_hi, a_lo, b_hi, b_lo):
                pe.matmul(dst, a_hi, b_hi, start=True, stop=False)
                pe.matmul(dst, a_hi, b_lo, start=False, stop=False)
                return pe.matmul(dst, a_lo, b_hi, start=False, stop=True)

            pe.wait_ge(consts_ready, CONSTS)
            pe.wait_ge(w_loaded, 16 * 8)
            for i in range(4):
                ins = turn(side_tiles(0)[:, i, :], wqkvo_raw[:, i, :], ident[:])
            ins.then_inc(w_turned, 1)
            pe.matmul(side(1)[:, 0:E * KH + 3], vec_raw, ident[0:E * KH + 3, 0:E * KH + 3],
                      start=True, stop=True).then_inc(w_turned, 1)

            def xT(bb, c, bank=0):
                pe.wait_ge(xn_ready, 2 * bb + c + 1)
                for t in range(TH):
                    ins = turn(side_tiles(bank)[:, t, :], xn[:, c * TH + t, :], ident[:])
                ins.then_inc(xT_done, 1)

            def qk_proj(bb, i, bank=0):
                c = i % 2
                pe.wait_ge(xT_lo_ready, 2 * bb + c + 1)
                three(side(bank), wqkv_hi[:, i // 2, :], wqkv_lo[:, i // 2, :], xT_hi[:, c, :],
                      xT_lo[:, c, :]).then_inc(qk_proj_done, 1)

            def v_proj(bb, c, bank=0):
                for t in range(TH):
                    ins = three(side_tiles(bank)[:, t, :], xT_hi[:, c, t * P:t * P + P], xT_lo[:, c, t * P:t * P + P],
                                wqkv_hi[:, 2, :], wqkv_lo[:, 2, :])
                ins.then_inc(v_proj_done, 1)

            def scores(b, par, s):
                k, half = s % T, s // T
                if s == 0:
                    pe.wait_ge(stacked, 16 * STACKS * (b + 1))
                for u in range(2):
                    wait(pe, clip_done, 2 * STEPS * b + 2 * s + u - 1)
                    for h in (2 * u, 2 * u + 1):
                        ins = pe.matmul(score_ps[:, h, :], kstack[:, par, h, k * P:k * P + P],
                                        qstack[:, par, h, half * HALF:half * HALF + HALF], start=True, stop=True)
                    ins.then_inc(qk_done, 1)

            def sums(b, par, s):
                k, g, G = s % T, STEPS * b + s, GROUPS * b + s // GROUP
                j = s % GROUP
                if s == 0:
                    pe.wait_ge(v_ready, 2 * b + 2)
                pe.wait_ge(exp_done, 2 * g + 2)
                wait(pe, ctx_copied, g - 1)

                def contexts():
                    for h in range(HEADS):
                        head = slice(DH * h, DH * h + DH)
                        ins = pe.matmul(sum_ps[head, s % 2, :], v_sb[:, par, k, head], probs[:, s % 2, h, :],
                                        start=True, stop=True, tile_position=(0, DH * h))
                    ins.then_inc(ctx_done, 1)

                def denominators():
                    if j == 0:
                        wait(pe, rinv_ready, G)
                    for c in range(2):
                        for h in range(HEADS):
                            ins = pe.matmul(den_ps[DH * h:DH * h + DH, :], gather[:, c, j, :],
                                            probs[:, s % 2, h, c * (HALF // 2):(c + 1) * (HALF // 2)],
                                            start=(j == 0 and c == 0), stop=(j == GROUP - 1 and c == 1),
                                            tile_position=(0, DH * h))
                    ins.then_inc(den_added, 1)

                if j == GROUP - 1:
                    denominators()
                    contexts()
                else:
                    contexts()
                    denominators()

            def wo(n):
                pe.wait_ge(ctxT_ready, n + 1)
                for t in range(TH):
                    ins = pe.matmul(side_tiles(0)[:, t, :], ctxT[:, t * P:t * P + P], woT[:], start=True, stop=True)
                ins.then_inc(wo_done, 1)

            pe.wait_ge(w_split, 5)
            pe.wait_ge(w_low, 1)
            for c in range(2):
                xT(0, c, c)
            for i in range(4):
                if i >= 2:
                    pe.wait_ge(qk_ready, i - 1)
                qk_proj(0, i, i % 2)
            for c in range(2):
                pe.wait_ge(qk_ready, 3 + c)
                v_proj(0, c, c)
            pe.wait_ge(mask_made, T)
            for k in range(T):
                if k < 2:
                    pe.wait_ge(v_ready, k + 1)
                else:
                    pe.wait_ge(limit_ready, k - 1)
                for t in range(T):
                    ins = turn(side(k % 2).bitcast(BF16)[:, t * P:t * P + P], mask20[:, t, k, :], identb[:])
                ins.then_inc(mask_turned, 1)
            scores(0, 0, 0)

            def body(b, par=None):
                par = b % 2 if par is None else par
                first, last = isinstance(b, int) and b == 0, isinstance(b, int) and b == LAST
                m, n, bb = 2 * b - 1, 2 * b, b + 1
                for s in range(STEPS):
                    if s + 1 < STEPS:
                        scores(b, par, s + 1)
                    elif not last:
                        scores(b + 1, 1 - par, 0)
                    if s == 0 and first:
                        pe.wait_ge(limit_ready, T)
                    if not last:
                        if s == 3:
                            wait(pe, res_ready, m)
                            xT(bb, 0)
                        if s == 4:
                            pe.wait_ge(xT_lo_ready, 2 * bb + 1)
                            xT(bb, 1)
                        if s in (5, 6, 7, 8):
                            if s == 5:
                                pe.wait_ge(xT_lo_ready, 2 * bb + 2)
                            else:
                                pe.wait_ge(qk_ready, 4 * bb + s - 5)
                            qk_proj(bb, s - 5)
                    if s == 11 and not first:
                        if last:
                            pe.wait_ge(res_ready, m)
                        else:
                            pe.wait_ge(qk_ready, 4 * bb + 4)
                        wo(m)
                    if s == 12 and not last:
                        if first:
                            pe.wait_ge(qk_ready, 4 * bb + 4)
                        else:
                            pe.wait_ge(res_ready, m + 1)
                        v_proj(bb, 0)
                    if s == 13 and not last:
                        pe.wait_ge(v_ready, 2 * bb + 1)
                        v_proj(bb, 1)
                    if s == 1 and not first:
                        pe.wait_ge(v_ready, 2 * b + 2)
                        wo(n - 2)
                    sums(b, par, s)

            bodies(pe, body)
            pe.wait_ge(res_ready, 2 * LAST)
            wo(2 * LAST)

            def x2T(b, half):
                c = 2 * b + half
                pe.wait_ge((xn2_even_ready, xn2_odd_ready)[half], b + 1)
                wait(pe, x2T_lo_ready, c - 1)
                for t in range(TH):
                    ins = turn(sum_ps[:, half, t * P:t * P + P], xn2[:, half, t, :], ident[:])
                ins.then_inc(x2T_done, 1)

            def gate(c):
                pe.wait_ge(x2T_lo_ready, c + 1)
                for t in range(TH):
                    ins = three(logits_ps[:, c, t * E:t * E + E], x2T_hi[:, c, t * P:t * P + P],
                                x2T_lo[:, c, t * P:t * P + P], gate_hi[:], gate_lo[:])
                ins.then_inc(gate_done, 1)

            def turn_cw(c, half):
                pe.wait_ge(cw_copied, c + 1)
                wait(pe, cwT_ready, c)
                for t in range(TH):
                    ins = turn(side(1)[0:E, t * P:t * P + P], cw[:, half, t, :], ident[:])
                ins.then_inc(cwT_done, 1)

            def weighted_b2(c):
                pe.wait_ge(cwT_ready, c + 1)
                wait(pe, acc_start, c)
                for t in range(TH):
                    ins = pe.matmul(side_tiles(0)[:, t, :], cwT[:, t * P:t * P + P], b2_sb[:], start=True, stop=True)
                ins.then_inc(b2_done, 1)

            def hidden(c, u):
                n = E * c + u
                wait(pe, gelu_done, 2 * n - 2)
                for k in range(KH):
                    three(score_ps[:, 2 * (u % 2) + k, :], w1_hi[:, u, k * P:k * P + P], w1_lo[:, u, k * P:k * P + P],
                          x2T_hi[:, c, :], x2T_lo[:, c, :]).then_inc(z_done, 1)

            def second(c, u):
                n = E * c + u
                pe.wait_ge(hid_lo_ready, 2 * n + 2)
                wait(pe, acc_done, n - 1)
                for t in range(TH):
                    for k in range(KH):
                        cols = slice(t * P, t * P + P)
                        hi, lo = hid_hi[:, u % 4, k, cols], hid_lo[:, u % 4, k, cols]
                        dst = sum_ps[:, u % 2, cols]
                        pe.matmul(dst, hi, w2_hi[:, u, k, :], start=(k == 0), stop=False)
                        pe.matmul(dst, hi, w2_lo[:, u, k, :], start=False, stop=False)
                        ins = pe.matmul(dst, lo, w2_hi[:, u, k, :], start=False, stop=(k == KH - 1))
                ins.then_inc(y_done, 1)

            pe.wait_ge(ctx_copied, STEPS * NB)
            pe.wait_ge(clip_done, 2 * STEPS * NB)
            pe.wait_ge(gate_step, 3)
            pe.wait_ge(ffn_step, 6)
            def turn_rows(b):
                x2T(b, 0)
                x2T(b, 1)
                if not (isinstance(b, int) and b == 0):
                    gate(2 * b - 2)
                    gate(2 * b - 1)

            turn_rows(0)
            with pe.Fori(1, MIDDLE) as b:
                turn_rows(b)
            pe.wait_ge(res_ready, 2 * LAST + 1)
            wo(2 * LAST + 1)
            with pe.Fori(MIDDLE, LAST) as b:
                turn_rows(b)
            gate(2 * LAST - 2)
            gate(2 * LAST - 1)
            x2T(LAST, 0)
            x2T(LAST, 1)
            pe.wait_ge(gate_dve, 1)
            gate(2 * LAST)
            gate(2 * LAST + 1)
            pe.wait_ge(gate_dve, GATE_OPS + 1)
            pe.wait_ge(res_ready, 2 * NB)
            hidden(0, 0)
            hidden(0, 1)
            turn_cw(0, 0)
            weighted_b2(0)

            def body_b(b, par=None):
                for half in range(2):
                    c = 2 * b + half
                    final = half == 1 and isinstance(b, int) and b == LAST
                    for u in range(E):
                        if u + 2 < E:
                            hidden(c, u + 2)
                        elif not final:
                            hidden(c + 1, u + 2 - E)
                        if not final:
                            if u == 3:
                                turn_cw(c + 1, 1 - half)
                            if u == 6:
                                weighted_b2(c + 1)
                        second(c, u)

            bodies(pe, body_b)


_INS = ["x", "adj", "L0_gnn_Wq", "L0_gnn_bq", "L0_gnn_Wk", "L0_gnn_bk", "L0_gnn_Wv", "L0_gnn_bv", "L0_gnn_Wo",
        "L0_gnn_bo", "L0_gnn_gamma", "L0_gnn_beta", "L0_ffn_gate_w", "L0_ffn_gate_b", "L0_ffn_W1", "L0_ffn_b1",
        "L0_ffn_W2", "L0_ffn_b2"]


def kernel(**inputs):
    import numpy as np
    import concourse.bacc as bacc
    from concourse.bass_utils import run_bass_kernel_spmd

    nc = bacc.Bacc("TRN2", target_bir_lowering=False, num_devices=1)
    arrays, args = {}, []
    for name in _INS:
        a = np.ascontiguousarray(inputs[name])
        arrays[f"in_{name}"] = a
        args.append(nc.dram_tensor(f"in_{name}", a.shape, mybir.dt.from_np(a.dtype), kind="ExternalInput").ap())
    out = nc.dram_tensor("out_x", inputs["x"].shape, F32, kind="ExternalOutput").ap()
    gnn_moe(nc, *args, out)
    r = run_bass_kernel_spmd(nc, [arrays], core_ids=[0])
    return r.results[0]["out_x"]
```
